# Optimizing a Trainium2 kernel written in Bass

```python
import numpy as np
import jax
import jax.numpy as jnp

def _softmax(x, axis=-1):
    return jax.nn.softmax(x, axis=axis)

def _gelu(x):
    return jax.nn.gelu(x, approximate=True)

def _silu(x):
    return jax.nn.silu(x)

def _sigmoid(x):
    return jax.nn.sigmoid(x)

def _layernorm(x, axis=-1, eps=1e-05):
    m = jnp.mean(x, axis=axis, keepdims=True)
    v = jnp.var(x, axis=axis, keepdims=True)
    return (x - m) / jnp.sqrt(v + eps)

def _scatter_add(tgt, idx, src, axis=0):
    return tgt.at[idx].add(src)

def _segment_sum(src, seg, n):
    return jax.ops.segment_sum(src, seg, n)
kernel_name = 'mk_gnn_preln_d2_gnn_r8_0f2cad'

def setup_inputs(seed: int=0):
    np.random.seed(seed)
    _w = jnp.asarray

    def _rec_inputs():
        import jax
        import jax.numpy as jnp
        _gk = jax.random.key(seed)
        x = -0.000202 + 1 * jax.random.normal(jax.random.fold_in(_gk, 1), (12500, 64), jnp.float32)
        _s = jax.random.randint(jax.random.fold_in(_gk, 2), (200000,), 0, 12500, jnp.int32)
        _d = jax.random.randint(jax.random.fold_in(_gk, 3), (200000,), 0, 12500, jnp.int32)
        _loop = jnp.arange(12500, dtype=jnp.int32)
        src = jnp.concatenate([_s, _d, _loop])
        dst = jnp.concatenate([_d, _s, _loop])
        _o = jnp.argsort(dst, stable=True)
        src = src[_o]
        dst = dst[_o]
        edge_attr_64 = -6.74381e-05 + 0.999835 * jax.random.normal(jax.random.fold_in(_gk, 12), (412500, 64), jnp.float32)
        edge_type_10 = jax.random.randint(jax.random.fold_in(_gk, 14), (412500,), 0, 10, jnp.int32)
        edge_type_8 = jax.random.randint(jax.random.fold_in(_gk, 15), (412500,), 0, 8, jnp.int32)
        return (x, src, dst, edge_attr_64, edge_type_10, edge_type_8)
    x, src, dst, edge_attr_64, edge_type_10, edge_type_8 = _rec_inputs()

    def _L0_gnn_setup():
        import jax, jax.numpy as jnp
        import numpy as np
        NEG_SLOPE = 0.01
        N_NODES = 12500
        N_EDGES = 156250
        N_REL = 10
        D = 64
        key = jax.random.key(seed)
        ks = jax.random.split(key, 8)
        return {'nfeat': jax.random.normal(ks[0], (N_NODES, D), dtype=jnp.float32), 'efeat': jax.random.normal(ks[1], (N_EDGES, D), dtype=jnp.float32), 'relation_weight': jax.random.normal(ks[2], (N_REL, D, D), dtype=jnp.float32) * (1.0 / np.sqrt(D)), 'res_fc_w': jax.random.normal(ks[3], (D, D), dtype=jnp.float32) * (1.0 / np.sqrt(D)), 'res_fc2_w': jax.random.normal(ks[4], (D, D), dtype=jnp.float32) * (1.0 / np.sqrt(D)), 'src': jax.random.randint(ks[5], (N_EDGES,), 0, N_NODES, dtype=jnp.int32), 'dst': jnp.sort(jax.random.randint(ks[6], (N_EDGES,), 0, N_NODES, dtype=jnp.int32)), 'etype': jax.random.randint(ks[7], (N_EDGES,), 0, N_REL, dtype=jnp.int32)}
    _L0_gnn_all = _L0_gnn_setup()
    _L0_gnn_in = {k: v for k, v in _L0_gnn_all.items() if k in ('relation_weight', 'res_fc_w', 'res_fc2_w')}
    del _L0_gnn_all

    def _L1_gnn_setup():
        import jax, jax.numpy as jnp
        import numpy as np
        N_NODES = 6250
        N_EDGES = 200000
        D = 64
        R = 8

        def _rgcn_layer(x, edge_index, edge_type, W, root, bias):
            src, dst = (edge_index[0], edge_index[1])
            h = jnp.einsum('nd,rdf->rnf', x, W)
            msg = h[edge_type, src]
            agg = jax.ops.segment_sum(msg, dst, num_segments=x.shape[0])
            return agg + x @ root + bias
        key = jax.random.key(seed)
        ks = jax.random.split(key, 9)
        adj = jax.random.randint(ks[0], (2, N_EDGES), 0, N_NODES, dtype=jnp.int32)
        features = jax.random.normal(ks[1], (N_NODES, D), dtype=jnp.float32)
        edge_type = jax.random.randint(ks[2], (N_EDGES,), 0, R, dtype=jnp.int32)
        s = 1.0 / np.sqrt(D)
        W1 = jax.random.normal(ks[3], (R, D, D), dtype=jnp.float32) * s
        root1 = jax.random.normal(ks[4], (D, D), dtype=jnp.float32) * s
        b1 = jnp.zeros((D,), dtype=jnp.float32)
        W2 = jax.random.normal(ks[5], (R, D, D), dtype=jnp.float32) * s
        root2 = jax.random.normal(ks[6], (D, D), dtype=jnp.float32) * s
        b2 = jnp.zeros((D,), dtype=jnp.float32)
        return {'adj': adj, 'features': features, 'edge_type': edge_type, 'W1': W1, 'root1': root1, 'b1': b1, 'W2': W2, 'root2': root2, 'b2': b2}
    _L1_gnn_all = _L1_gnn_setup()
    _L1_gnn_in = {k: v for k, v in _L1_gnn_all.items() if k in ('W1', 'root1', 'b1', 'W2', 'root2', 'b2')}
    del _L1_gnn_all
    return {'x': x, 'src': src, 'dst': dst, 'edge_attr_64': edge_attr_64, 'edge_type_10': edge_type_10, 'edge_type_8': edge_type_8, 'L0_gnn_relation_weight': _L0_gnn_in['relation_weight'], 'L0_gnn_res_fc_w': _L0_gnn_in['res_fc_w'], 'L0_gnn_res_fc2_w': _L0_gnn_in['res_fc2_w'], 'L1_gnn_W1': _L1_gnn_in['W1'], 'L1_gnn_root1': _L1_gnn_in['root1'], 'L1_gnn_b1': _L1_gnn_in['b1'], 'L1_gnn_W2': _L1_gnn_in['W2'], 'L1_gnn_root2': _L1_gnn_in['root2'], 'L1_gnn_b2': _L1_gnn_in['b2']}

def reference(x, src, dst, edge_attr_64, edge_type_10, edge_type_8, L0_gnn_relation_weight, L0_gnn_res_fc_w, L0_gnn_res_fc2_w, L1_gnn_W1, L1_gnn_root1, L1_gnn_b1, L1_gnn_W2, L1_gnn_root2, L1_gnn_b2):
    import jax
    import jax.numpy as jnp

    def _L0_gnn_ref(nfeat, efeat, relation_weight, res_fc_w, res_fc2_w, src, dst, etype):
        import jax, jax.numpy as jnp
        import numpy as np
        NEG_SLOPE = 0.01
        N_NODES = 12500
        N_EDGES = 156250
        N_REL = 10
        D = 64
        n = nfeat.shape[0]
        proj = jnp.einsum('ni,rio->nro', nfeat, relation_weight)
        t_r = proj[src, etype]
        h_r = proj[dst, etype]
        att = jnp.sum(t_r * jnp.tanh(h_r + efeat), axis=-1)
        seg_max = jax.ops.segment_max(att, dst, num_segments=n)
        ex = jnp.exp(att - seg_max[dst])
        seg_sum = jax.ops.segment_sum(ex, dst, num_segments=n)
        a = ex / seg_sum[dst]
        h_nb = jax.ops.segment_sum(nfeat[src] * a[:, None], dst, num_segments=n)
        out = jax.nn.leaky_relu((nfeat + h_nb) @ res_fc_w.T, NEG_SLOPE) + jax.nn.leaky_relu(nfeat * h_nb @ res_fc2_w.T, NEG_SLOPE)
        return out

    def _L1_gnn_ref(adj, features, edge_type, W1, root1, b1, W2, root2, b2):
        import jax, jax.numpy as jnp
        import numpy as np
        N_NODES = 6250
        N_EDGES = 200000
        D = 64
        R = 8

        def _rgcn_layer(x, edge_index, edge_type, W, root, bias):
            src, dst = (edge_index[0], edge_index[1])
            h = jnp.einsum('nd,rdf->rnf', x, W)
            msg = h[edge_type, src]
            agg = jax.ops.segment_sum(msg, dst, num_segments=x.shape[0])
            return agg + x @ root + bias
        x = _rgcn_layer(features, adj, edge_type, W1, root1, b1)
        x = jax.nn.relu(x)
        x = _rgcn_layer(x, adj, edge_type, W2, root2, b2)
        return x
    edge_index = jnp.stack([src, dst])
    h = jnp.maximum(_layernorm(x, axis=-1), 0.0)
    x = x + _L0_gnn_ref(h, edge_attr_64, L0_gnn_relation_weight, L0_gnn_res_fc_w, L0_gnn_res_fc2_w, src, dst, edge_type_10)
    h = jnp.maximum(_layernorm(x, axis=-1), 0.0)
    x = x + _L1_gnn_ref(edge_index, h, edge_type_8, L1_gnn_W1, L1_gnn_root1, L1_gnn_b1, L1_gnn_W2, L1_gnn_root2, L1_gnn_b2)
    return x

_drawn_inputs = setup_inputs


def setup_inputs(seed=0):
    import zlib

    import numpy as np

    out = dict(_drawn_inputs(seed))
    spreads = {'L1_gnn_b1': (0.0, 0.661), 'L1_gnn_b2': (0.0, 2.0)}
    factors = {}
    for name, (base, spread) in spreads.items():
        noise = np.random.default_rng([zlib.crc32(name.encode()), seed]).standard_normal(out[name].shape)
        drawn = base * np.exp(spread * noise) if base else spread * noise
        out[name] = jnp.asarray(drawn.astype(out[name].dtype))
    for name, factor in factors.items():
        out[name] = (out[name] * factor).astype(out[name].dtype)
    return out
```

```python
from contextlib import ExitStack

import concourse.bass as bass
from concourse import mybir

F32 = mybir.dt.float32
I32 = mybir.dt.int32
ALU = mybir.AluOpType
ACT = mybir.ActivationFunctionType
AX = mybir.AxisListType
RMAX = bass.bass_isa.ReduceOp.max

P = 128
D = 64
BT = 8
BE = BT * P
W = 64
SLOTS = 4
NEG_MASK = -1e30
NEG_START = -1e28
TINY = 1e-30
LN_EPS = 1e-5
LEAK = 0.01


class Shapes:

    def __init__(self, n_nodes, n_edges, r0, r1):
        self.N, self.E, self.R0, self.R1 = n_nodes, n_edges, r0, r1
        self.NT = 2 * -(-n_nodes // (2 * P))
        self.NPAD = self.NT * P
        self.NWIN = max(self.NPAD, n_nodes + W)
        self.NREAL = -(-n_edges // BE)
        self.OVERLAP = self.NREAL * BE - n_edges
        self.ROUNDS = -(-self.NREAL // SLOTS)
        self.NB = self.ROUNDS * SLOTS


class Item:

    def __init__(self, i, k, slots, done, used):
        self.i, self.k, self.slots, self.done, self.used = i, k, slots, done, used
        self.slot, self.bank = k % slots, k % 2
        self.number = i * slots + k

    def exists(self, among=None):
        n = self.number
        return not isinstance(n, int) or (n >= 0 and (among is None or n < among))

    def first_use(self):
        return isinstance(self.number, int) and self.number < self.slots

    def count(self):
        return self.done + (self.k + 1)

    def slot_count(self, each):
        return (self.used + (self.k // self.slots + 1)) * each

    def back(self, lag):
        return Item(self.i, self.k - lag, self.slots, self.done, self.used)


def each_block(eng, sh, passes, step, drain=0, at_end=None):
    with eng.Fori(0, passes) as j:
        done, used = eng.snap(j * sh.NB), eng.snap(j * sh.ROUNDS)
        for k in range(SLOTS):
            step(Item(0, k, SLOTS, done, used))
        with eng.Fori(1, sh.ROUNDS - 1) as i:
            done, used = eng.snap(j * sh.NB + i * SLOTS), eng.snap(j * sh.ROUNDS + i)
            for k in range(SLOTS):
                step(Item(i, k, SLOTS, done, used))
        done = eng.snap(j * sh.NB + (sh.NB - SLOTS))
        used = eng.snap(j * sh.ROUNDS + (sh.ROUNDS - 1))
        for k in range(SLOTS + drain):
            step(Item(sh.ROUNDS - 1, k, SLOTS, done, used))
        if at_end:
            at_end(j)


def each_tile(eng, sh, step, drain=0, peeled=1):
    last = sh.NT // 2 - 1
    for i in range(peeled):
        for k in range(2):
            step(Item(i, k, 2, i * 2, i))
    with eng.Fori(peeled, last) as i:
        for k in range(2):
            step(Item(i, k, 2, i * 2, i))
    for k in range(2 + drain):
        step(Item(last, k, 2, last * 2, last))


def constants(nc, sem, m):
    s_zero, s_const = sem("ident_zeroed"), sem("constants_ready")
    with nc.Block() as block:
        @block.gpsimd
        def _(pool):
            nc.gpsimd.memset(m.ident[:, :], 0.0).then_inc(s_zero, 1)
            pool.wait_ge(s_zero, 1)
            nc.gpsimd.affine_select(out=m.ident[:, :], in_=m.ident[:, :], compare_op=ALU.not_equal, fill=1.0,
                                    base=0, pattern=[[-1, P]], channel_multiplier=1).then_inc(s_const, 1)
            nc.gpsimd.iota(m.iota[:, :], pattern=[[1, W]], base=0, channel_multiplier=0,
                           allow_small_or_imprecise_dtypes=True).then_inc(s_const, 1)
            nc.gpsimd.memset(m.ones[:, :], 1.0).then_inc(s_const, 1)
            pool.wait_ge(s_const, 3)


def edge_indices(nc, sem, sh, m, src, dst, type0, type1):
    NG = -(-sh.NB // P)
    rows_of = [min(P, sh.NB - g * P) for g in range(NG)]
    real_of = [min(n, sh.NREAL - 1 - g * P) for g, n in enumerate(rows_of)]
    loads_of = [4 * ((r > 0) + (n - r)) * 16 for n, r in zip(rows_of, real_of)]
    loaded, indexed, masked, turned = sem("idx_loaded"), sem("idx_made"), sem("idx_masked"), sem("idx_turned")
    taken = [sem("idx_taken_v"), sem("idx_taken_s")]
    stored, bounds, spans_ready = sem("idx_stored"), sem("idx_bounds"), sem("idx_spans")
    span_lane, span_all_ready, span_int, spread = (sem("idx_" + x) for x in (
        "span_lane", "span_all", "span_int", "spread"))
    with ExitStack() as local:
        def sb(name, shape, dt):
            return local.enter_context(nc.sbuf_tensor(name, shape, dt))

        raw = [sb(f"raw_{n}", [P, BE], I32) for n in ("src", "dst", "type0", "type1")]
        val = sb("val", [P, 4, BE], F32)
        rows_i = sb("rows_i", [P, P, 3, BT], I32)
        rows_d = sb("rows_d", [P, P, BT], F32)
        bmin, bmax, span1, span_all = (sb(n, [P, 1], F32) for n in ("bmin", "bmax", "span1", "span_all"))
        bmin_i = sb("bmin_i", [P, 1], I32)
        spans = sb("spans", [P, NG], F32)
        ps = [local.enter_context(nc.psum_tensor(f"ps_turn{n}", [P, 4, P], F32)) for n in range(2)]

        def take(eng, copy, g, t):
            n = rows_of[g]
            eng.wait_ge(turned, BT * g + t + 1)
            if g:
                eng.wait_ge(stored, 64 * g)
            copy(rows_i[:, 0:n, :, t], ps[t % 2][:, 0:3, 0:n].rearrange("p a b -> p b a")).then_inc(taken[t % 2], 1)
            copy(rows_d[:, 0:n, t], ps[t % 2][:, 3, 0:n]).then_inc(taken[t % 2], 1)

        with nc.Block() as block:
            @block.sync
            def _(sp):
                for g in range(NG):
                    n, real = rows_of[g], real_of[g]
                    if g:
                        sp.wait_ge(indexed, 4 * g)
                    for t, a in zip(raw, (src, dst, type0, type1)):
                        if real > 0:
                            sp.dma_start(t[0:real, :], a[g * P * BE:(g * P + real) * BE].rearrange(
                                "(b e) -> b e", e=BE)).then_inc(loaded, 16)
                        for row in range(real, n):
                            sp.dma_start(t[row:row + 1, :], a[sh.E - BE:sh.E].rearrange("(b e) -> b e", e=BE)
                                         ).then_inc(loaded, 16)
                    sp.wait_ge(bounds, 2 * (g + 1))
                    sp.dma_start(m.base_i_dram[g * P:g * P + n, :], bmin_i[0:n, :]).then_inc(stored, 16)
                    sp.dma_start(m.base_f_dram[g * P:g * P + n, :], bmin[0:n, :]).then_inc(stored, 16)
                    for s in taken:
                        sp.wait_ge(s, BT * (g + 1))
                    sp.dma_start(m.rows_dram[g * P:g * P + n, :, :].rearrange("b p c -> p b c"),
                                 rows_i[:, 0:n, :, :].rearrange("p b a t -> p b (a t)")).then_inc(stored, 16)
                    sp.dma_start(m.dst_dram[g * P:g * P + n, :, :].rearrange("b p c -> p b c"),
                                 rows_d[:, 0:n, :]).then_inc(stored, 16)
                    sp.wait_ge(stored, 64 * (g + 1))
                sp.dma_start(m.base_f[:, :], m.base_f_dram.rearrange("b a -> (b a)").partition_broadcast(P)
                             ).then_inc(spread, 16)
                sp.dma_start(m.base_i[:, :], m.base_i_dram.rearrange("b a -> a b")).then_inc(spread, 16)
                sp.wait_ge(spread, 32)

            @block.vector
            def _(dve):
                v = nc.vector
                v.memset(spans[:, :], 0.0).then_inc(spans_ready, 1)
                dve.wait_ge(spans_ready, 1)
                arrived = 0
                for g in range(NG):
                    n = rows_of[g]
                    arrived += loads_of[g]
                    dve.wait_ge(loaded, arrived)
                    if g:
                        dve.wait_ge(turned, BT * g)
                        dve.wait_ge(stored, 64 * g)
                    r_src, r_dst, r_t0, r_t1 = (t[0:n, :] for t in raw)
                    v.scalar_tensor_tensor(val[0:n, 0, :], r_src, float(sh.R0), r_t0, ALU.mult, ALU.add
                                           ).then_inc(indexed, 1)
                    v.scalar_tensor_tensor(val[0:n, 1, :], r_dst, float(sh.R0), r_t0, ALU.mult, ALU.add
                                           ).then_inc(indexed, 1)
                    v.scalar_tensor_tensor(val[0:n, 2, :], r_src, float(sh.R1), r_t1, ALU.mult, ALU.add
                                           ).then_inc(indexed, 1)
                    v.tensor_copy(val[0:n, 3, :], r_dst).then_inc(indexed, 1)
                    dve.wait_ge(indexed, 4 * (g + 1))
                    v.tensor_reduce(bmin[0:n, :], val[0:n, 3, :], AX.X, ALU.min).then_inc(bounds, 1)
                    v.tensor_reduce(bmax[0:n, :], val[0:n, 3, :], AX.X, ALU.max).then_inc(spans_ready, 1)
                    dve.wait_ge(bounds, 2 * g + 1)
                    v.tensor_copy(bmin_i[0:n, :], bmin[0:n, :]).then_inc(bounds, 1)
                    dve.wait_ge(spans_ready, 2 + 2 * g)
                    v.tensor_tensor(spans[0:n, g:g + 1], bmax[0:n, :], bmin[0:n, :], ALU.subtract
                                    ).then_inc(spans_ready, 1)
                    for t in range(0, BT, 2):
                        take(dve, v.tensor_copy, g, t)
                dve.wait_ge(spans_ready, 1 + 2 * NG)
                v.tensor_reduce(span1[:, :], spans[:, :], AX.X, ALU.max).then_inc(span_lane, 1)
                dve.wait_ge(span_all_ready, 1)
                v.tensor_copy(m.span_i[:, :], span_all[0:1, :]).then_inc(span_int, 1)
                dve.wait_ge(span_int, 1)

            @block.scalar
            def _(act):
                for g in range(NG):
                    for t in range(1, BT, 2):
                        take(act, nc.scalar.copy, g, t)

            @block.gpsimd
            def _(pool):
                g = NG - 1
                pool.wait_ge(bounds, 2 * g + 1)
                pool.wait_ge(spans_ready, 2 + 2 * g)
                part = val[0:rows_of[g], 3, :]
                nc.gpsimd.affine_select(out=part, in_=part, compare_op=ALU.is_ge, fill=-1.0,
                                        base=real_of[g] * BE - sh.OVERLAP, pattern=[[1, BE]],
                                        channel_multiplier=-BE).then_inc(masked, 1)
                pool.wait_ge(span_lane, 1)
                nc.gpsimd.partition_all_reduce(span_all[:, :], span1[:, :], P, RMAX).then_inc(span_all_ready, 1)

            @block.tensor
            def _(pe):
                for g in range(NG):
                    n = rows_of[g]
                    pe.wait_ge(indexed, 4 * (g + 1))
                    if g == NG - 1:
                        pe.wait_ge(masked, 1)
                    for t in range(BT):
                        tile = BT * g + t
                        if tile >= 2:
                            pe.wait_ge(taken[t % 2], 2 * (tile // 2))
                        for a in range(4):
                            last = nc.tensor.transpose(ps[t % 2][:, a, 0:n], val[0:n, a, t * P:(t + 1) * P],
                                                       m.ident[0:n, 0:n])
                        last.then_inc(turned, 1)


def load_nodes(eng, sh, dst, dram, loaded):
    whole = sh.N // P
    eng.dma_start(dst[:, 0:whole, :], dram[0:whole * P, :].rearrange("(t p) d -> p t d", p=P)).then_inc(loaded, 16)
    eng.dma_start(dst[0:sh.N - whole * P, whole, :], dram[whole * P:sh.N, :]).then_inc(loaded, 16)


def layernorm_relu(nc, sem, sh, name, h, x, scratch, x_dram=None, h_dram=None):
    cleared, loaded, made, root, kept = (sem(f"{name}_{x}") for x in ("cleared", "loaded", "made", "root", "kept"))
    with ExitStack() as local:
        def sb(what):
            return local.enter_context(nc.sbuf_tensor(f"{name}_{what}", [P, sh.NT], F32))

        mean, var, std, rstd = sb("mean"), sb("var"), sb("std"), sb("rstd")
        wide = [P, sh.NT, D]
        with nc.Block() as block:
            @block.sync
            def _(sp):
                if x_dram is not None:
                    sp.wait_ge(cleared, 1)
                    load_nodes(sp, sh, x, x_dram, loaded)
                if h_dram is not None:
                    sp.wait_ge(made, 7)
                    sp.dma_start(h_dram.rearrange("(t p) d -> p t d", p=P), h[:, :, :]).then_inc(kept, 16)
                    sp.wait_ge(kept, 16)

            @block.vector
            def _(dve):
                v = nc.vector
                if x_dram is not None:
                    v.memset(x[:, sh.N // P:sh.NT, :], 0.0).then_inc(cleared, 1)
                    dve.wait_ge(loaded, 32)
                v.tensor_reduce(mean[:, :], x[:, :, :], AX.X, ALU.add).then_inc(made, 1)
                dve.wait_ge(made, 1)
                v.scalar_tensor_tensor(h[:, :, :], mean[:, :].unsqueeze(2).to_broadcast(wide), -1.0 / D, x[:, :, :],
                                       ALU.mult, ALU.add).then_inc(made, 1)
                dve.wait_ge(made, 2)
                v.tensor_tensor(scratch[:, :, :], h[:, :, :], h[:, :, :], ALU.mult).then_inc(made, 1)
                dve.wait_ge(made, 3)
                v.tensor_reduce(var[:, :], scratch[:, :, :], AX.X, ALU.add).then_inc(made, 1)
                dve.wait_ge(made, 4)
                v.tensor_scalar(std[:, :], var[:, :], 1.0 / D, LN_EPS, ALU.mult, ALU.add).then_inc(made, 1)
                dve.wait_ge(root, 1)
                v.reciprocal(rstd[:, :], std[:, :]).then_inc(made, 1)
                dve.wait_ge(made, 6)
                v.scalar_tensor_tensor(h[:, :, :], h[:, :, :], 0.0, rstd[:, :].unsqueeze(2).to_broadcast(wide),
                                       ALU.max, ALU.mult).then_inc(made, 1)
                dve.wait_ge(made, 7)

            @block.scalar
            def _(act):
                act.wait_ge(made, 5)
                nc.scalar.activation(std[:, :], std[:, :], ACT.Sqrt).then_inc(root, 1)


def relation_table(nc, sem, sh, m, name, table, weights, n_rel, h=None, with_h=False, root=None, bias=None):
    wide = (2 * D) if with_h else D
    off = wide - D
    per_bank = n_rel // 2 if n_rel * D > 512 else n_rel
    banks = n_rel // per_bank
    w_in, staged, turned, ht_ready, projected, rooted = (sem(f"{name}_{x}") for x in (
        "weights", "staged", "turned", "ht", "projected", "rooted"))
    sums_ready, rows_ready, copies_ready = (sem(f"{name}_{x}") for x in ("sums", "rows", "copies"))
    stored = [sem(f"{name}_stored{q}") for q in range(2)]
    n_w = 16 * (1 if root is None else 3)
    with ExitStack() as local:
        def sb(what, shape):
            return local.enter_context(nc.sbuf_tensor(f"{name}_{what}", shape, F32))

        w = sb("w", [D, n_rel, D])
        w_root, b_root = sb("w_root", [D, D]), sb("b_root", [D, 1])
        ht = sb("ht", [D, 2, P])
        h_tile = sb("h_tile", [P, 2, D])
        rows = sb("rows", [P, 2, n_rel, wide])
        ps_t = [local.enter_context(nc.psum_tensor(f"{name}_ps_t{q}", [D, 512], F32)) for q in range(2)]
        ps_w = [[local.enter_context(nc.psum_tensor(f"{name}_ps_w{q}{b}", [P, 512], F32)) for b in range(banks)]
                for q in range(2)]
        ps_r = [local.enter_context(nc.psum_tensor(f"{name}_ps_r{q}", [D, 512], F32)) for q in range(2)] if root is not None else None

        with nc.Block() as block:
            @block.sync
            def _(sp):
                sp.dma_start(w[:, :, :], weights.rearrange("r i o -> i r o")).then_inc(w_in, 16)
                if root is not None:
                    sp.dma_start(w_root[:, :], root).then_inc(w_in, 16)
                    sp.dma_start(b_root[:, :], bias.rearrange("(o a) -> o a", a=1)).then_inc(w_in, 16)

                def step(t):
                    sp.wait_ge(rows_ready, t.count())
                    if with_h:
                        sp.wait_ge(copies_ready, t.count())
                    sp.dma_start(table[bass.ds(t.number * P, P), :, :], rows[:, t.slot, :, :]
                                 ).then_inc(stored[t.slot], 16)

                each_tile(sp, sh, step)
                for s in stored:
                    sp.wait_ge(s, 16 * (sh.NT // 2))

            if h is not None:
                @block.gpsimd
                def _(pool):
                    each_tile(pool, sh, lambda t: stage_tile(
                        nc, pool, sh, m, t, h_tile, h[:, bass.ds(t.number, 1), :].rearrange("p a d -> p (a d)"),
                        staged, turned))

            @block.tensor
            def _(pe):
                pe.wait_ge(w_in, n_w)

                def step(t):
                    if h is not None and t.exists(sh.NT):
                        if t.back(2).exists():
                            pe.wait_ge(ht_ready, t.back(2).count())
                        pe.wait_ge(staged, t.count())
                        hold(pe, m)
                        nc.tensor.transpose(ps_t[t.slot][:, 0:P], h_tile[:, t.slot, :], m.ident[:, :]
                                            ).then_inc(turned, 1)
                    t = t.back(1)
                    if t.exists():
                        pe.wait_ge(ht_ready, t.count())
                        if t.back(2).exists():
                            pe.wait_ge(rows_ready, t.back(2).count())
                        for b in range(banks):
                            last = nc.tensor.matmul(
                                ps_w[t.slot][b][:, 0:per_bank * D], ht[:, t.slot, :],
                                w[:, b * per_bank:(b + 1) * per_bank, :].rearrange("i r o -> i (r o)"),
                                start=True, stop=True)
                        last.then_inc(projected, 1)
                        if root is not None:
                            if t.back(2).exists():
                                pe.wait_ge(sums_ready, t.back(2).count())
                            hold(pe, m)
                            nc.tensor.matmul(ps_r[t.slot][:, 0:P], w_root[:, :], ht[:, t.slot, :],
                                             start=True, stop=True).then_inc(rooted, 1)

                each_tile(pe, sh, step, drain=1)

            @block.scalar
            def _(act):
                if root is not None:
                    act.wait_ge(w_in, n_w)

                def step(t):
                    if t.exists(sh.NT):
                        if t.back(2).exists():
                            act.wait_ge(projected, t.back(2).count())
                            if root is not None:
                                act.wait_ge(rooted, t.back(2).count())
                        cols = bass.ds(t.number * P, P)
                        if h is not None:
                            act.wait_ge(turned, t.count())
                            nc.scalar.copy(ht[:, t.slot, :], ps_t[t.slot][:, 0:P]).then_inc(ht_ready, 1)
                        else:
                            hold(act, m)
                            nc.scalar.activation(ht[:, t.slot, :], m.sums[0:D, cols], ACT.Relu).then_inc(ht_ready, 1)
                        if with_h:
                            if t.back(2).exists():
                                act.wait_ge(stored[t.slot], t.back(2).slot_count(16))
                            hold(act, m)
                            nc.scalar.copy(rows[:, t.slot, :, 0:D], h[:, bass.ds(t.number, 1), :].to_broadcast(
                                [P, n_rel, D])).then_inc(copies_ready, 1)
                    t = t.back(1)
                    if root is not None and t.exists():
                        act.wait_ge(rooted, t.count())
                        hold(act, m)
                        nc.scalar.activation(m.sums[0:D, bass.ds(t.number * P, P)], ps_r[t.slot][:, 0:P],
                                             ACT.Identity, bias=b_root[:, :]).then_inc(sums_ready, 1)

                each_tile(act, sh, step, drain=1 if root is not None else 0)

            @block.vector
            def _(dve):
                def step(t):
                    dve.wait_ge(projected, t.count())
                    if t.back(2).exists():
                        dve.wait_ge(stored[t.slot], t.back(2).slot_count(16))
                    for b in range(banks):
                        last = nc.vector.tensor_copy(
                            rows[:, t.slot, b * per_bank:(b + 1) * per_bank, off:wide],
                            ps_w[t.slot][b][:, 0:per_bank * D].rearrange("p (r o) -> p r o", o=D))
                    last.then_inc(rows_ready, 1)

                each_tile(dve, sh, step)


def hold(eng, m):
    eng.sem_inc(m.held)


def stage_tile(nc, pool, sh, m, t, slots, source, staged, used):
    if t.back(2).exists():
        pool.wait_ge(used, t.back(2).count())
        hold(pool, m)
    nc.gpsimd.tensor_copy(slots[:, t.slot, :], source).then_inc(staged, 1)


def passes_of(eng, m):
    span = eng.value_load(m.span_i[0:1, 0:1], min_val=0, max_val=m.max_span)
    return eng.snap(span // W + 1)


def next_windows(nc, dve, sh, m, moved, j):
    nc.vector.tensor_scalar(m.base_f[:, :], m.base_f[:, :], float(W), float(sh.N), ALU.add, ALU.min
                            ).then_inc(moved, 1)
    nc.vector.tensor_scalar(m.base_i[:, :], m.base_i[:, :], W, sh.N, ALU.add, ALU.min).then_inc(moved, 1)
    dve.wait_ge(moved, (j + 1) * 2)


def first_windows(nc, sem, m, name):
    spread = sem(f"{name}_windows")
    with nc.Block() as block:
        @block.sync
        def _(sp):
            sp.dma_start(m.base_f[:, :], m.base_f_dram.rearrange("b a -> (b a)").partition_broadcast(P)
                         ).then_inc(spread, 16)
            sp.dma_start(m.base_i[:, :], m.base_i_dram.rearrange("b a -> a b")).then_inc(spread, 16)
            sp.wait_ge(spread, 32)


def attention_edges(nc, sem, sh, m, table, edge_attr):
    loaded = [sem(f"att_loaded{q}") for q in range(SLOTS)]
    src_in = [sem(f"att_src_in{q}") for q in range(SLOTS)]
    dst_in = [sem(f"att_dst_in{q}") for q in range(SLOTS)]
    (cleared, pre_ready, tanh_ready, prod_ready, score_ready, unlike_ready, masked_ready, lane_max_ready,
     max_turned, node_max_ready, diag_ready, max_spread, new_max_ready, drop_ready, kept_ready, shifted_ready,
     weight_ready, scale_ready, summed, scaled, added, moved) = (sem("att_" + x) for x in (
         "cleared", "pre", "tanh", "prod", "score", "unlike", "masked", "lane_max", "max_turned",
         "node_max", "diag", "max_spread", "new_max", "drop", "kept", "shifted", "weight", "scale", "summed",
         "scaled", "added", "moved"))
    flat_table = table.rearrange("n r d -> (n r) d")
    with ExitStack() as local:
        def sb(name, shape, dt=F32):
            return local.enter_context(nc.sbuf_tensor(name, shape, dt))

        def psum(name):
            return [local.enter_context(nc.psum_tensor(f"{name}{q}", [P, 512], F32)) for q in range(2)]

        run_max = sb("run_max", [P, sh.NWIN])
        rows = sb("att_rows", [P, SLOTS, 3, BT], I32)
        dst = sb("att_dst", [P, SLOTS, BT])
        from_src = sb("from_src", [P, SLOTS, BT, 3 * D])
        from_dst = sb("from_dst", [P, SLOTS, BT, 2 * D])
        edge = sb("edge", [P, SLOTS, BT, D])
        score = sb("score", [P, SLOTS, BT])
        wgt = sb("wgt", [P, SLOTS, BT, W])
        lane_max = sb("lane_max", [P, SLOTS, W])
        node_max = sb("node_max", [W, SLOTS])
        diag = sb("diag", [W, SLOTS, W])
        new_max = sb("new_max", [P, SLOTS, W])
        drop = sb("drop", [P, SLOTS, W])
        ps_turn, ps_spread, ps_sum = psum("ps_turn_"), psum("ps_spread_"), psum("ps_sum_")

        tiles = [P, BT, W]

        with nc.Block() as block:
            @block.sync
            def _(sp):
                def step(b):
                    if not b.first_use():
                        sp.wait_ge(masked_ready, b.back(SLOTS).count())
                    sp.dma_start(rows[:, b.slot, :, :].rearrange("p a t -> p (a t)"),
                                 m.rows_dram[bass.ds(b.number, 1), :, :].rearrange("b p c -> p (b c)")
                                 ).then_inc(loaded[b.slot], 16)
                    sp.dma_start(dst[:, b.slot, :], m.dst_dram[bass.ds(b.number, 1), :, :].rearrange(
                        "b p c -> p (b c)")).then_inc(loaded[b.slot], 16)
                    first = b.number * BE
                    if isinstance(first, int):
                        first = min(first, sh.E - BE)
                    sp.dma_start(edge[:, b.slot, :, :], edge_attr[bass.ds(first, BE), :].rearrange(
                        "(t p) d -> p t d", p=P)).then_inc(loaded[b.slot], 16)

                each_block(sp, sh, passes_of(sp, m), step,
                           at_end=lambda j: sp.wait_ge(masked_ready, (j + 1) * sh.NB))

            @block.gpsimd
            def _(pool):
                pool.wait_ge(cleared, 3)

                def step(b):
                    if not b.first_use():
                        pool.wait_ge(summed, b.back(SLOTS).count())
                    pool.wait_ge(loaded[b.slot], b.slot_count(48))
                    hold(pool, m)
                    for t in range(BT):
                        nc.gpsimd.indirect_dma_start(
                            out=from_dst[:, b.slot, t, :], out_offset=None, in_=flat_table,
                            in_offset=bass.IndirectOffsetOnAxis(ap=rows[:, b.slot, 1, t:t + 1], axis=0)
                        ).then_inc(dst_in[b.slot], 16)
                    for t in range(BT):
                        nc.gpsimd.indirect_dma_start(
                            out=from_src[:, b.slot, t, D:3 * D], out_offset=None, in_=flat_table,
                            in_offset=bass.IndirectOffsetOnAxis(ap=rows[:, b.slot, 0, t:t + 1], axis=0)
                        ).then_inc(src_in[b.slot], 16)

                each_block(pool, sh, passes_of(pool, m), step,
                           at_end=lambda j: pool.wait_ge(summed, (j + 1) * sh.NB))

            @block.vector
            def _(dve):
                v = nc.vector
                v.memset(from_src[:, :, :, 0:D], 1.0).then_inc(cleared, 1)
                v.memset(run_max[:, :], NEG_START).then_inc(cleared, 1)
                v.memset(m.sums[:, :], 0.0).then_inc(cleared, 1)
                dve.wait_ge(cleared, 3)

                def window(b):
                    base = dve.value_load(m.base_i[0:1, bass.ds(b.number, 1)], min_val=0, max_val=sh.N)
                    return bass.ds(base, W)

                def node_maximum(b):
                    dve.wait_ge(max_turned, b.count())
                    v.tensor_reduce(node_max[:, b.slot:b.slot + 1], ps_turn[b.bank][0:W, 0:P], AX.X, ALU.max
                                    ).then_inc(node_max_ready, 1)
                    dve.wait_ge(node_max_ready, b.count())
                    v.tensor_scalar(diag[:, b.slot, :], m.ident[0:W, 0:W], node_max[:, b.slot:b.slot + 1], None,
                                    ALU.mult).then_inc(diag_ready, 1)

                def scores(b):
                    wg = wgt[:, b.slot, :, :]
                    v.scalar_tensor_tensor(wg, dst[:, b.slot, :].unsqueeze(2).to_broadcast(tiles),
                                           m.base_f[:, bass.ds(b.number, 1)],
                                           m.iota[:, :].unsqueeze(1).to_broadcast(tiles),
                                           ALU.subtract, ALU.not_equal).then_inc(unlike_ready, 1)
                    dve.wait_ge(tanh_ready, b.count())
                    dve.wait_ge(src_in[b.slot], b.slot_count(16 * BT))
                    e = edge[:, b.slot, :, :]
                    v.tensor_tensor(e, e, from_src[:, b.slot, :, 2 * D:3 * D], ALU.mult).then_inc(prod_ready, 1)
                    dve.wait_ge(prod_ready, b.count())
                    v.tensor_reduce(score[:, b.slot, :], e, AX.X, ALU.add).then_inc(score_ready, 1)
                    dve.wait_ge(score_ready, b.count())
                    dve.wait_ge(unlike_ready, b.count())
                    v.scalar_tensor_tensor(wg, wg, NEG_MASK, score[:, b.slot, :].unsqueeze(2).to_broadcast(tiles),
                                           ALU.mult, ALU.add).then_inc(masked_ready, 1)
                    dve.wait_ge(masked_ready, b.count())
                    v.tensor_reduce(lane_max[:, b.slot, :], wg.rearrange("p t w -> p w t"), AX.X, ALU.max
                                    ).then_inc(lane_max_ready, 1)

                def add_sums(b):
                    part = m.sums[:, window(b)]
                    if b.back(1).exists():
                        dve.wait_ge(added, b.back(1).count())
                    dve.wait_ge(scale_ready, b.count())
                    v.tensor_tensor(part, part, drop[:, b.slot, :], ALU.mult).then_inc(scaled, 1)
                    dve.wait_ge(scaled, b.count())
                    dve.wait_ge(summed, b.count())
                    v.tensor_tensor(part, part, ps_sum[b.bank][:, 0:W], ALU.add).then_inc(added, 1)

                def new_maximum(b):
                    part = run_max[:, window(b)]
                    if b.back(1).exists():
                        dve.wait_ge(kept_ready, b.back(1).count())
                    dve.wait_ge(max_spread, b.count())
                    v.tensor_tensor(new_max[:, b.slot, :], part, ps_spread[b.bank][:, 0:W], ALU.max
                                    ).then_inc(new_max_ready, 1)
                    dve.wait_ge(new_max_ready, b.count())
                    v.tensor_tensor(drop[:, b.slot, :], part, new_max[:, b.slot, :], ALU.subtract
                                    ).then_inc(drop_ready, 1)
                    wg = wgt[:, b.slot, :, :]
                    v.tensor_tensor(wg, wg, new_max[:, b.slot, :].unsqueeze(1).to_broadcast(tiles), ALU.subtract
                                    ).then_inc(shifted_ready, 1)
                    dve.wait_ge(drop_ready, b.count())
                    v.tensor_tensor(part, part, new_max[:, b.slot, :], ALU.max).then_inc(kept_ready, 1)

                def before_tanh(b):
                    dve.wait_ge(loaded[b.slot], b.slot_count(48))
                    dve.wait_ge(dst_in[b.slot], b.slot_count(16 * BT))
                    e = edge[:, b.slot, :, :]
                    v.tensor_tensor(e, e, from_dst[:, b.slot, :, D:2 * D], ALU.add).then_inc(pre_ready, 1)

                def is_real(b):
                    return b.exists(sh.NB)

                def step(b):
                    for stage, lag in ((node_maximum, 2), (scores, 1), (add_sums, 3), (new_maximum, 2),
                                       (before_tanh, 0)):
                        if is_real(b.back(lag)):
                            stage(b.back(lag))

                def end_of_pass(j):
                    next_windows(nc, dve, sh, m, moved, j)

                each_block(dve, sh, passes_of(dve, m), step, drain=3, at_end=end_of_pass)

            @block.scalar
            def _(act):
                def step(b):
                    p = b.back(2)
                    if p.exists():
                        act.wait_ge(shifted_ready, p.count())
                        nc.scalar.activation(wgt[:, p.slot, :, :], wgt[:, p.slot, :, :], ACT.Exp
                                             ).then_inc(weight_ready, 1)
                        act.wait_ge(drop_ready, p.count())
                        nc.scalar.activation(drop[:, p.slot, :], drop[:, p.slot, :], ACT.Exp
                                             ).then_inc(scale_ready, 1)
                    if b.exists(sh.NB):
                        act.wait_ge(pre_ready, b.count())
                        nc.scalar.activation(edge[:, b.slot, :, :], edge[:, b.slot, :, :], ACT.Tanh
                                             ).then_inc(tanh_ready, 1)

                each_block(act, sh, passes_of(act, m), step, drain=2)

            @block.tensor
            def _(pe):
                def step(b):
                    p = b.back(2)
                    if p.exists():
                        pe.wait_ge(diag_ready, p.count())
                        if p.back(2).exists():
                            pe.wait_ge(new_max_ready, p.back(2).count())
                        nc.tensor.matmul(ps_spread[p.bank][:, 0:W], m.ones[0:W, :], diag[:, p.slot, :],
                                         start=True, stop=True).then_inc(max_spread, 1)
                    q = b.back(1)
                    if q.exists(sh.NB):
                        pe.wait_ge(lane_max_ready, q.count())
                        if q.back(2).exists():
                            pe.wait_ge(node_max_ready, q.back(2).count())
                        hold(pe, m)
                        nc.tensor.transpose(ps_turn[q.bank][0:W, 0:P], lane_max[:, q.slot, :], m.ident[:, :]
                                            ).then_inc(max_turned, 1)
                    if p.exists():
                        pe.wait_ge(weight_ready, p.count())
                        if p.back(2).exists():
                            pe.wait_ge(added, p.back(2).count())
                        for t in range(BT):
                            last = nc.tensor.matmul(ps_sum[p.bank][:, 0:W], from_src[:, p.slot, t, 0:2 * D],
                                                    wgt[:, p.slot, t, :], start=(t == 0), stop=(t == BT - 1))
                        last.then_inc(summed, 1)

                each_block(pe, sh, passes_of(pe, m), step, drain=2)


def attention_output(nc, sem, sh, m, x, h, fc1, fc2):
    (w_zero, w_in, w_turned, w_ready, staged, turned, den_ready, inv_ready, nb_ready, pair_ready, pair_turned, pair_copied,
     mixed, leak_ready, kept, half_ready, x_ready) = (sem("out0_" + x) for x in (
         "w_zero", "w_in", "w_turned", "w_ready", "staged", "turned", "den", "inv", "nb", "pair", "pair_turned",
         "pair_copied", "mixed", "leak", "kept", "half", "x"))
    with ExitStack() as local:
        def sb(name, shape):
            return local.enter_context(nc.sbuf_tensor(name, shape, F32))

        def psum(name):
            return [local.enter_context(nc.psum_tensor(f"{name}{q}", [P, 512], F32)) for q in range(2)]

        w_raw, w = sb("fc_raw", [P, P]), sb("fc", [P, P])
        den, inv = sb("den", [P, 2]), sb("inv", [P, 2])
        nb = sb("nb", [P, 2, D])
        sums_tile = sb("sums_tile", [P, 2, P])
        pair, pair_t = sb("pair", [P, 2, 2 * D]), sb("pair_t", [P, 2, P])
        leak = sb("leak", [P, 2, 2 * D])
        ps_n, ps_p, ps_m = psum("ps_nodes"), psum("ps_pair"), psum("ps_mixed")
        with nc.Block() as block:
            @block.sync
            def _(sp):
                sp.wait_ge(w_zero, 1)
                sp.dma_start(w_raw[0:D, 0:D], fc1).then_inc(w_in, 16)
                sp.dma_start(w_raw[D:P, D:P], fc2).then_inc(w_in, 16)

            @block.gpsimd
            def _(pool):
                each_tile(pool, sh, lambda t: stage_tile(nc, pool, sh, m, t, sums_tile,
                                                         m.sums[:, bass.ds(t.number * P, P)], staged, turned))

            @block.tensor
            def _(pe):
                pe.wait_ge(w_in, 32)
                nc.tensor.transpose(ps_m[0][:, 0:P], w_raw[:, :], m.ident[:, :]).then_inc(w_turned, 1)
                pe.wait_ge(w_ready, 1)

                def step(t):
                    if t.exists(sh.NT):
                        if t.back(2).exists():
                            pe.wait_ge(nb_ready, t.back(2).count())
                        pe.wait_ge(staged, t.count())
                        nc.tensor.transpose(ps_n[t.slot][:, 0:P], sums_tile[:, t.slot, :], m.ident[:, :]
                                            ).then_inc(turned, 1)
                    a = t.back(1)
                    if a.exists(sh.NT):
                        pe.wait_ge(pair_ready, a.count() * 2)
                        if a.back(2).exists():
                            pe.wait_ge(pair_copied, a.back(2).count())
                        nc.tensor.transpose(ps_p[a.slot][:, 0:P], pair[:, a.slot, :], m.ident[:, :]
                                            ).then_inc(pair_turned, 1)
                    b = t.back(2)
                    if b.exists():
                        pe.wait_ge(pair_copied, b.count())
                        if b.back(2).exists():
                            pe.wait_ge(kept, b.back(2).count())
                        nc.tensor.matmul(ps_m[b.slot][:, 0:P], pair_t[:, b.slot, :], w[:, :], start=True, stop=True
                                         ).then_inc(mixed, 1)

                each_tile(pe, sh, step, drain=2, peeled=2)

            @block.scalar
            def _(act):
                act.wait_ge(w_turned, 1)
                nc.scalar.copy(w[:, :], ps_m[0][:, 0:P]).then_inc(w_ready, 1)

                def step(t):
                    a = t.back(1)
                    if a.exists(sh.NT):
                        act.wait_ge(pair_turned, a.count())
                        if a.back(2).exists():
                            act.wait_ge(mixed, a.back(2).count())
                        nc.scalar.copy(pair_t[:, a.slot, :], ps_p[a.slot][:, 0:P]).then_inc(pair_copied, 1)
                    b = t.back(2)
                    if b.exists():
                        act.wait_ge(mixed, b.count())
                        if b.back(2).exists():
                            act.wait_ge(kept, b.back(2).count())
                        nc.scalar.mul(leak[:, b.slot, :], ps_m[b.slot][:, 0:P], LEAK).then_inc(leak_ready, 1)

                each_tile(act, sh, step, drain=2, peeled=2)

            @block.vector
            def _(dve):
                v = nc.vector
                v.memset(w_raw[:, :], 0.0).then_inc(w_zero, 1)

                def neighbours(t):
                    q = t.slot
                    hh = h[:, bass.ds(t.number, 1), :].rearrange("p a d -> p (a d)")
                    dve.wait_ge(turned, t.count())
                    v.tensor_scalar(den[:, q:q + 1], ps_n[q][:, 0:1], TINY, None, ALU.max).then_inc(den_ready, 1)
                    dve.wait_ge(den_ready, t.count())
                    v.reciprocal(inv[:, q:q + 1], den[:, q:q + 1]).then_inc(inv_ready, 1)
                    dve.wait_ge(inv_ready, t.count())
                    v.tensor_scalar(nb[:, q, :], ps_n[q][:, D:2 * D], inv[:, q:q + 1], None, ALU.mult
                                    ).then_inc(nb_ready, 1)
                    dve.wait_ge(nb_ready, t.count())
                    if t.back(2).exists():
                        dve.wait_ge(pair_turned, t.back(2).count())
                    v.tensor_tensor(pair[:, q, 0:D], hh, nb[:, q, :], ALU.add).then_inc(pair_ready, 1)
                    v.tensor_tensor(pair[:, q, D:2 * D], hh, nb[:, q, :], ALU.mult).then_inc(pair_ready, 1)

                def residual(t):
                    q = t.slot
                    xx = x[:, bass.ds(t.number, 1), :].rearrange("p a d -> p (a d)")
                    dve.wait_ge(leak_ready, t.count())
                    v.tensor_tensor(leak[:, q, :], leak[:, q, :], ps_m[q][:, 0:P], ALU.max).then_inc(half_ready, 1)
                    dve.wait_ge(half_ready, t.count())
                    v.tensor_tensor(xx, xx, leak[:, q, 0:D], ALU.add).then_inc(x_ready, 1)
                    dve.wait_ge(x_ready, t.count())
                    v.tensor_tensor(xx, xx, leak[:, q, D:2 * D], ALU.add).then_inc(kept, 1)

                def step(t):
                    if t.exists(sh.NT):
                        neighbours(t)
                    if t.back(2).exists():
                        residual(t.back(2))

                each_tile(dve, sh, step, drain=2, peeled=2)
                dve.wait_ge(kept, sh.NT)


def relation_edges(nc, sem, sh, m, name, table):
    loaded = [sem(f"{name}_loaded{q}") for q in range(SLOTS)]
    src_in = [sem(f"{name}_src_in{q}") for q in range(SLOTS)]
    alike_ready, summed, added, moved = (sem(f"{name}_{x}") for x in (
        "alike", "summed", "added", "moved"))
    flat_table = table.rearrange("n r d -> (n r) d")
    with ExitStack() as local:
        def sb(what, shape, dt=F32):
            return local.enter_context(nc.sbuf_tensor(f"{name}_{what}", shape, dt))

        rows = sb("rows", [P, SLOTS, 3, BT], I32)
        dst = sb("dst", [P, SLOTS, BT])
        msg = sb("msg", [P, SLOTS, BT, D])
        alike = sb("alike", [P, SLOTS, BT, W])
        ps_sum = [local.enter_context(nc.psum_tensor(f"{name}_ps{q}", [D, 512], F32)) for q in range(2)]
        tiles = [P, BT, W]

        with nc.Block() as block:
            @block.sync
            def _(sp):
                def step(b):
                    if not b.first_use():
                        sp.wait_ge(summed, b.back(SLOTS).count())
                    sp.dma_start(rows[:, b.slot, :, :].rearrange("p a t -> p (a t)"),
                                 m.rows_dram[bass.ds(b.number, 1), :, :].rearrange("b p c -> p (b c)")
                                 ).then_inc(loaded[b.slot], 16)
                    sp.dma_start(dst[:, b.slot, :], m.dst_dram[bass.ds(b.number, 1), :, :].rearrange(
                        "b p c -> p (b c)")).then_inc(loaded[b.slot], 16)

                each_block(sp, sh, passes_of(sp, m), step, at_end=lambda j: sp.wait_ge(summed, (j + 1) * sh.NB))

            @block.gpsimd
            def _(pool):
                def step(b):
                    if not b.first_use():
                        pool.wait_ge(summed, b.back(SLOTS).count())
                    pool.wait_ge(loaded[b.slot], b.slot_count(32))
                    hold(pool, m)
                    for t in range(BT):
                        nc.gpsimd.indirect_dma_start(
                            out=msg[:, b.slot, t, :], out_offset=None, in_=flat_table,
                            in_offset=bass.IndirectOffsetOnAxis(ap=rows[:, b.slot, 2, t:t + 1], axis=0)
                        ).then_inc(src_in[b.slot], 16)

                each_block(pool, sh, passes_of(pool, m), step,
                           at_end=lambda j: pool.wait_ge(summed, (j + 1) * sh.NB))

            @block.vector
            def _(dve):
                def one_hot(b):
                    dve.wait_ge(loaded[b.slot], b.slot_count(32))
                    nc.vector.scalar_tensor_tensor(
                        alike[:, b.slot, :, :], dst[:, b.slot, :].unsqueeze(2).to_broadcast(tiles),
                        m.base_f[:, bass.ds(b.number, 1)], m.iota[:, :].unsqueeze(1).to_broadcast(tiles),
                        ALU.subtract, ALU.is_equal).then_inc(alike_ready, 1)

                def add_sums(b):
                    base = dve.value_load(m.base_i[0:1, bass.ds(b.number, 1)], min_val=0, max_val=sh.N)
                    part = m.sums[0:D, bass.ds(base, W)]
                    if b.back(1).exists():
                        dve.wait_ge(added, b.back(1).count())
                    dve.wait_ge(summed, b.count())
                    nc.vector.tensor_tensor(part, part, ps_sum[b.bank][:, 0:W], ALU.add).then_inc(added, 1)

                def step(b):
                    if b.exists(sh.NB):
                        one_hot(b)
                    if b.back(1).exists():
                        add_sums(b.back(1))

                def end_of_pass(j):
                    next_windows(nc, dve, sh, m, moved, j)

                each_block(dve, sh, passes_of(dve, m), step, drain=1, at_end=end_of_pass)

            @block.tensor
            def _(pe):
                def step(b):
                    pe.wait_ge(alike_ready, b.count())
                    pe.wait_ge(src_in[b.slot], b.slot_count(16 * BT))
                    if b.back(2).exists():
                        pe.wait_ge(added, b.back(2).count())
                    for t in range(BT):
                        last = nc.tensor.matmul(ps_sum[b.bank][:, 0:W], msg[:, b.slot, t, :], alike[:, b.slot, t, :],
                                                start=(t == 0), stop=(t == BT - 1))
                    last.then_inc(summed, 1)

                each_block(pe, sh, passes_of(pe, m), step)


def output(nc, sem, sh, m, x, out):
    staged, turned, ready, stored = (sem("out_" + x) for x in ("staged", "turned", "ready", "stored"))
    with ExitStack() as local:
        sums_tile = local.enter_context(nc.sbuf_tensor("sums_tile_out", [D, 2, P], F32))
        ps = [local.enter_context(nc.psum_tensor(f"out_ps{q}", [P, 512], F32)) for q in range(2)]
        with nc.Block() as block:
            @block.gpsimd
            def _(pool):
                each_tile(pool, sh, lambda t: stage_tile(nc, pool, sh, m, t, sums_tile,
                                                         m.sums[0:D, bass.ds(t.number * P, P)], staged, turned))

            @block.tensor
            def _(pe):
                def step(t):
                    if t.back(2).exists():
                        pe.wait_ge(ready, t.back(2).count())
                    pe.wait_ge(staged, t.count())
                    hold(pe, m)
                    nc.tensor.transpose(ps[t.slot][:, 0:D], sums_tile[:, t.slot, :],
                                        m.ident[0:D, 0:D]).then_inc(turned, 1)

                each_tile(pe, sh, step)

            @block.vector
            def _(dve):
                def step(t):
                    dve.wait_ge(turned, t.count())
                    xx = x[:, bass.ds(t.number, 1), :].rearrange("p a d -> p (a d)")
                    nc.vector.tensor_tensor(xx, xx, ps[t.slot][:, 0:D], ALU.add).then_inc(ready, 1)

                each_tile(dve, sh, step)

            @block.sync
            def _(sp):
                sp.wait_ge(ready, sh.NT)
                whole = sh.N // P
                sp.dma_start(out[0:whole * P, :].rearrange("(t p) d -> p t d", p=P), x[:, 0:whole, :]
                             ).then_inc(stored, 16)
                sp.dma_start(out[whole * P:sh.N, :], x[0:sh.N - whole * P, whole, :]).then_inc(stored, 16)
                sp.wait_ge(stored, 32)


class Shared:
    pass


def build(nc, x, src, dst, edge_attr, type0, type1, w_rel, fc1, fc2, w1, root1, b1, w2, root2, b2, out):
    sh = Shapes(x.shape[0], src.shape[0], w_rel.shape[0], w1.shape[0])
    m = Shared()
    m.max_span = sh.N - 1
    m.rows_dram = nc.dram_tensor("edge_rows", (sh.NB, P, 3 * BT), I32, kind="Internal").ap()
    m.dst_dram = nc.dram_tensor("edge_dst", (sh.NB, P, BT), F32, kind="Internal").ap()
    m.base_i_dram = nc.dram_tensor("base_int", (sh.NB, 1), I32, kind="Internal").ap()
    m.base_f_dram = nc.dram_tensor("base_float", (sh.NB, 1), F32, kind="Internal").ap()
    table0 = nc.dram_tensor("table0", (sh.NPAD, sh.R0, 2 * D), F32, kind="Internal").ap()
    table1 = nc.dram_tensor("table1", (sh.NPAD, sh.R1, D), F32, kind="Internal").ap()
    h_dram = nc.dram_tensor("h0", (sh.NPAD, D), F32, kind="Internal").ap()

    with ExitStack() as ctx:
        def sem(name):
            return ctx.enter_context(nc.semaphore(name))

        def sb(name, shape, dt=F32):
            return ctx.enter_context(nc.sbuf_tensor(name, shape, dt))

        m.held = sem("held")
        m.ident, m.ones, m.iota = sb("ident", [P, P]), sb("ones", [P, P]), sb("iota", [P, W])
        m.base_i, m.base_f = sb("base_i", [1, sh.NB], I32), sb("base_f", [P, sh.NB])
        m.span_i = sb("span_i", [1, 1], I32)
        wide = [P, sh.NT, D]

        constants(nc, sem, m)
        edge_indices(nc, sem, sh, m, src, dst, type0, type1)
        with nc.sbuf_tensor("x_a", wide, F32) as x_a, nc.sbuf_tensor("h_a", wide, F32) as h_a, \
                nc.sbuf_tensor("sq_a", wide, F32) as sq_a:
            layernorm_relu(nc, sem, sh, "ln0", h_a, x_a, sq_a, x_dram=x, h_dram=h_dram)
            relation_table(nc, sem, sh, m, "tab0", table0, w_rel, sh.R0, h=h_a, with_h=True)
        m.sums = sb("sums", [P, sh.NWIN])
        attention_edges(nc, sem, sh, m, table0, edge_attr)

        x_b = sb("x_b", wide)
        with nc.sbuf_tensor("h_b", wide, F32) as h_b, nc.sbuf_tensor("sq_b", wide, F32) as sq_b:
            reloaded = sem("reloaded")
            x_clear = sem("x_clear")
            with nc.Block() as block:
                @block.vector
                def _(dve):
                    nc.vector.memset(x_b[:, sh.N // P:sh.NT, :], 0.0).then_inc(x_clear, 1)

                @block.sync
                def _(sp):
                    sp.dma_start(h_b[:, :, :], h_dram.rearrange("(t p) d -> p t d", p=P)).then_inc(reloaded, 16)
                    sp.wait_ge(x_clear, 1)
                    load_nodes(sp, sh, x_b, x, reloaded)
                    sp.wait_ge(reloaded, 48)
            attention_output(nc, sem, sh, m, x_b, h_b, fc1, fc2)
            layernorm_relu(nc, sem, sh, "ln1", h_b, x_b, sq_b)
            first_windows(nc, sem, m, "conv1")
            relation_table(nc, sem, sh, m, "tab1", table1, w1, sh.R1, h=h_b, root=root1, bias=b1)
        relation_edges(nc, sem, sh, m, "conv1", table1)
        first_windows(nc, sem, m, "conv2")
        relation_table(nc, sem, sh, m, "tab2", table1, w2, sh.R1, root=root2, bias=b2)
        relation_edges(nc, sem, sh, m, "conv2", table1)
        output(nc, sem, sh, m, x_b, out)


_INS = ["x", "src", "dst", "edge_attr_64", "edge_type_10", "edge_type_8", "L0_gnn_relation_weight",
        "L0_gnn_res_fc_w", "L0_gnn_res_fc2_w", "L1_gnn_W1", "L1_gnn_root1", "L1_gnn_b1", "L1_gnn_W2",
        "L1_gnn_root2", "L1_gnn_b2"]


def kernel(**inputs):
    import numpy as _np
    import concourse.bacc as _bacc
    from concourse import mybir as _mybir
    from concourse.bass_utils import run_bass_kernel_spmd as _run

    nc = _bacc.Bacc("TRN2", target_bir_lowering=False, num_devices=1)
    arrays, args = {}, []
    for name in _INS:
        a = _np.ascontiguousarray(inputs[name])
        arrays[f"in_{name}"] = a
        args.append(nc.dram_tensor(f"in_{name}", a.shape, _mybir.dt.from_np(a.dtype), kind="ExternalInput").ap())
    out = nc.dram_tensor("out_0", inputs["x"].shape, _mybir.dt.float32, kind="ExternalOutput").ap()
    build(nc, *args, out)
    r = _run(nc, [arrays], core_ids=[0])
    return r.results[0]["out_0"]
```

```python
from contextlib import ExitStack

import concourse.bass as bass
from concourse import mybir

F32 = mybir.dt.float32
I32 = mybir.dt.int32
BF16 = mybir.dt.bfloat16
ALU = mybir.AluOpType
ACT = mybir.ActivationFunctionType
AX = mybir.AxisListType
RMAX = bass.bass_isa.ReduceOp.max

P = 128
D = 64
BT = 8
BE = BT * P
W = 64
SLOTS = 4
NEG_MASK = -1e30
NEG_START = -1e28
TINY = 1e-30
LN_EPS = 1e-5
LEAK = 0.01


class Shapes:

    def __init__(self, n_nodes, n_edges, r0, r1):
        self.N, self.E, self.R0, self.R1 = n_nodes, n_edges, r0, r1
        self.NT = 2 * -(-n_nodes // (2 * P))
        self.NPAD = self.NT * P
        self.NWIN = max(self.NPAD, n_nodes + W)
        self.NREAL = -(-n_edges // BE)
        self.OVERLAP = self.NREAL * BE - n_edges
        self.ROUNDS = -(-self.NREAL // SLOTS)
        self.NB = self.ROUNDS * SLOTS


class Item:

    def __init__(self, i, k, slots, done, used):
        self.i, self.k, self.slots, self.done, self.used = i, k, slots, done, used
        self.slot, self.bank = k % slots, k % 2
        self.number = i * slots + k

    def exists(self, among=None):
        n = self.number
        return not isinstance(n, int) or (n >= 0 and (among is None or n < among))

    def first_use(self):
        return isinstance(self.number, int) and self.number < self.slots

    def count(self):
        return self.done + (self.k + 1)

    def slot_count(self, each):
        return (self.used + (self.k // self.slots + 1)) * each

    def back(self, lag):
        return Item(self.i, self.k - lag, self.slots, self.done, self.used)


def each_block(eng, sh, passes, step, drain=0, peeled=1, at_end=None):
    with eng.Fori(0, passes) as j:
        for i in range(peeled):
            done, used = eng.snap(j * sh.NB + i * SLOTS), eng.snap(j * sh.ROUNDS + i)
            for k in range(SLOTS):
                step(Item(i, k, SLOTS, done, used))
        with eng.Fori(peeled, sh.ROUNDS - 1) as i:
            done, used = eng.snap(j * sh.NB + i * SLOTS), eng.snap(j * sh.ROUNDS + i)
            for k in range(SLOTS):
                step(Item(i, k, SLOTS, done, used))
        done = eng.snap(j * sh.NB + (sh.NB - SLOTS))
        used = eng.snap(j * sh.ROUNDS + (sh.ROUNDS - 1))
        for k in range(SLOTS + drain):
            step(Item(sh.ROUNDS - 1, k, SLOTS, done, used))
        if at_end:
            at_end(j)


def each_tile(eng, sh, step, drain=0, peeled=1):
    last = sh.NT // 2 - 1
    for i in range(peeled):
        for k in range(2):
            step(Item(i, k, 2, i * 2, i))
    with eng.Fori(peeled, last) as i:
        for k in range(2):
            step(Item(i, k, 2, i * 2, i))
    for k in range(2 + drain):
        step(Item(last, k, 2, last * 2, last))


def constants(nc, sem, m):
    s_zero, s_const = sem("ident_zeroed"), sem("constants_ready")
    with nc.Block() as block:
        @block.gpsimd
        def _(pool):
            nc.gpsimd.memset(m.ident[:, :], 0.0).then_inc(s_zero, 1)
            pool.wait_ge(s_zero, 1)
            nc.gpsimd.affine_select(out=m.ident[:, :], in_=m.ident[:, :], compare_op=ALU.not_equal, fill=1.0,
                                    base=0, pattern=[[-1, P]], channel_multiplier=1).then_inc(s_const, 1)
            nc.gpsimd.iota(m.iota[:, :], pattern=[[1, W]], base=0, channel_multiplier=0,
                           allow_small_or_imprecise_dtypes=True).then_inc(s_const, 1)
            nc.gpsimd.iota(m.lane[:, :], pattern=[[0, 1]], base=0, channel_multiplier=1,
                           allow_small_or_imprecise_dtypes=True).then_inc(s_const, 1)
            nc.gpsimd.memset(m.ones[:, :], 1.0).then_inc(s_const, 1)
            nc.gpsimd.memset(m.ones_bf[:, :], 1.0).then_inc(s_const, 1)
            pool.wait_ge(s_const, 5)


def edge_indices(nc, sem, sh, m, src, dst, type0, type1):
    NG = -(-sh.NB // P)
    rows_of = [min(P, sh.NB - g * P) for g in range(NG)]
    real_of = [min(n, sh.NREAL - 1 - g * P) for g, n in enumerate(rows_of)]
    loads_of = [4 * ((r > 0) + (n - r)) * 16 for n, r in zip(rows_of, real_of)]
    loaded, indexed, masked, turned = sem("idx_loaded"), sem("idx_made"), sem("idx_masked"), sem("idx_turned")
    taken = [sem("idx_taken_v"), sem("idx_taken_s")]
    stored, bounds, spans_ready = sem("idx_stored"), sem("idx_bounds"), sem("idx_spans")
    near_ready = sem("idx_near")
    span_lane, span_all_ready, span_int, spread = (sem("idx_" + x) for x in (
        "span_lane", "span_all", "span_int", "spread"))
    with ExitStack() as local:
        def sb(name, shape, dt):
            return local.enter_context(nc.sbuf_tensor(name, shape, dt))

        raw = [sb(f"raw_{n}", [P, BE], I32) for n in ("src", "dst", "type0", "type1")]
        val = sb("val", [P, 4, BE], F32)
        rows_i = sb("rows_i", [P, P, 4, BT], I32)
        bmin, bmax = sb("bmin", [P, 1], F32), sb("bmax", [P, 1], F32)
        span1, span_all = sb("span1", [P, 2], F32), sb("span_all", [P, 2], F32)
        bmin_i = sb("bmin_i", [P, 1], I32)
        spans = sb("spans", [P, 2, NG], F32)
        tbase, tbase_i = sb("tbase", [P, BT], F32), sb("tbase_i", [P, BT], I32)
        near, near_bf = sb("near", [P, BE], F32), sb("near_bf", [P, BE], BF16)
        ps = [local.enter_context(nc.psum_tensor(f"ps_turn{n}", [P, 4, P], F32)) for n in range(2)]

        def take(eng, copy, g, t):
            n = rows_of[g]
            eng.wait_ge(turned, BT * g + t + 1)
            if g:
                eng.wait_ge(stored, 80 * g)
            copy(rows_i[:, 0:n, 0:3, t], ps[t % 2][:, 0:3, 0:n].rearrange("p a b -> p b a")).then_inc(taken[t % 2], 1)
            copy(rows_i[:, 0:n, 3, t].bitcast(F32), ps[t % 2][:, 3, 0:n]).then_inc(taken[t % 2], 1)

        with nc.Block() as block:
            @block.sync
            def _(sp):
                for g in range(NG):
                    n, real = rows_of[g], real_of[g]
                    if g:
                        sp.wait_ge(indexed, 4 * g)
                    for t, a in zip(raw, (src, dst, type0, type1)):
                        if real > 0:
                            sp.dma_start(t[0:real, :], a[g * P * BE:(g * P + real) * BE].rearrange(
                                "(b e) -> b e", e=BE)).then_inc(loaded, 16)
                        for row in range(real, n):
                            sp.dma_start(t[row:row + 1, :], a[sh.E - BE:sh.E].rearrange("(b e) -> b e", e=BE)
                                         ).then_inc(loaded, 16)
                    sp.wait_ge(near_ready, 5 * (g + 1))
                    sp.dma_start(m.near_dram[g * P:g * P + n, :], near_bf[0:n, :]).then_inc(stored, 16)
                    sp.dma_start(m.near_base_dram[g * P:g * P + n, :], tbase_i[0:n, :]).then_inc(stored, 16)
                    sp.wait_ge(bounds, 2 * (g + 1))
                    sp.dma_start(m.base_i_dram[g * P:g * P + n, :], bmin_i[0:n, :]).then_inc(stored, 16)
                    sp.dma_start(m.base_f_dram[g * P:g * P + n, :], bmin[0:n, :]).then_inc(stored, 16)
                    for s in taken:
                        sp.wait_ge(s, BT * (g + 1))
                    sp.dma_start(m.rows_dram[g * P:g * P + n, :, :].rearrange("b p c -> p b c"),
                                 rows_i[:, 0:n, :, :].rearrange("p b a t -> p b (a t)")).then_inc(stored, 16)
                    sp.wait_ge(stored, 80 * (g + 1))
                sp.dma_start(m.base_f[:, :], m.base_f_dram.rearrange("b a -> (b a)").partition_broadcast(P)
                             ).then_inc(spread, 16)
                sp.dma_start(m.base_i[:, :], m.base_i_dram.rearrange("b a -> a b")).then_inc(spread, 16)
                sp.dma_start(m.near_base[:, :], m.near_base_dram.rearrange("(a b) t -> a (b t)", a=1)
                             ).then_inc(spread, 16)
                sp.wait_ge(spread, 48)

            @block.vector
            def _(dve):
                v = nc.vector
                v.memset(spans[:, :, :], 0.0).then_inc(spans_ready, 1)
                dve.wait_ge(spans_ready, 1)
                arrived = 0
                for g in range(NG):
                    n = rows_of[g]
                    arrived += loads_of[g]
                    dve.wait_ge(loaded, arrived)
                    if g:
                        dve.wait_ge(turned, BT * g)
                        dve.wait_ge(stored, 80 * g)
                    r_src, r_dst, r_t0, r_t1 = (t[0:n, :] for t in raw)
                    v.scalar_tensor_tensor(val[0:n, 0, :], r_src, float(sh.R0), r_t0, ALU.mult, ALU.add
                                           ).then_inc(indexed, 1)
                    v.scalar_tensor_tensor(val[0:n, 1, :], r_dst, float(sh.R0), r_t0, ALU.mult, ALU.add
                                           ).then_inc(indexed, 1)
                    v.scalar_tensor_tensor(val[0:n, 2, :], r_src, float(sh.R1), r_t1, ALU.mult, ALU.add
                                           ).then_inc(indexed, 1)
                    v.tensor_copy(val[0:n, 3, :], r_dst).then_inc(indexed, 1)
                    dve.wait_ge(indexed, 4 * (g + 1))
                    v.tensor_reduce(tbase[0:n, :], val[0:n, 3, :].rearrange("b (t p) -> b t p", p=P), AX.X, ALU.min
                                    ).then_inc(near_ready, 1)
                    v.tensor_reduce(bmax[0:n, :], val[0:n, 3, :], AX.X, ALU.max).then_inc(spans_ready, 1)
                    dve.wait_ge(near_ready, 5 * g + 1)
                    v.tensor_reduce(bmin[0:n, :], tbase[0:n, :], AX.X, ALU.min).then_inc(bounds, 1)
                    dve.wait_ge(bounds, 2 * g + 1)
                    v.tensor_copy(bmin_i[0:n, :], bmin[0:n, :]).then_inc(bounds, 1)
                    v.tensor_scalar(tbase[0:n, :], tbase[0:n, :], float(sh.R0), float(sh.NPAD * sh.R0 - P),
                                    ALU.mult, ALU.min).then_inc(near_ready, 1)
                    dve.wait_ge(near_ready, 5 * g + 2)
                    v.tensor_copy(tbase_i[0:n, :], tbase[0:n, :]).then_inc(near_ready, 1)
                    v.tensor_tensor(near[0:n, :].rearrange("b (t p) -> b t p", p=P),
                                    val[0:n, 1, :].rearrange("b (t p) -> b t p", p=P),
                                    tbase[0:n, :].unsqueeze(2).to_broadcast([n, BT, P]), ALU.subtract
                                    ).then_inc(near_ready, 1)
                    dve.wait_ge(near_ready, 5 * g + 4)
                    v.tensor_copy(near_bf[0:n, :], near[0:n, :]).then_inc(near_ready, 1)
                    dve.wait_ge(spans_ready, 2 + 3 * g)
                    v.tensor_tensor(spans[0:n, 0, g:g + 1], bmax[0:n, :], bmin[0:n, :], ALU.subtract
                                    ).then_inc(spans_ready, 1)
                    v.tensor_reduce(spans[0:n, 1, g:g + 1], near[0:n, :], AX.X, ALU.max).then_inc(spans_ready, 1)
                    for t in range(0, BT, 2):
                        take(dve, v.tensor_copy, g, t)
                dve.wait_ge(spans_ready, 1 + 3 * NG)
                v.tensor_reduce(span1[:, :], spans[:, :, :], AX.X, ALU.max).then_inc(span_lane, 1)
                dve.wait_ge(span_all_ready, 1)
                v.tensor_copy(m.span_i[:, :], span_all[0:1, :]).then_inc(span_int, 1)
                dve.wait_ge(span_int, 1)

            @block.scalar
            def _(act):
                for g in range(NG):
                    for t in range(1, BT, 2):
                        take(act, nc.scalar.copy, g, t)

            @block.gpsimd
            def _(pool):
                g = NG - 1
                pool.wait_ge(bounds, 2 * g + 1)
                pool.wait_ge(spans_ready, 2 + 3 * g)
                pool.wait_ge(near_ready, 5 * g + 1)
                part = val[0:rows_of[g], 3, :]
                nc.gpsimd.affine_select(out=part, in_=part, compare_op=ALU.is_ge, fill=-1.0,
                                        base=real_of[g] * BE - sh.OVERLAP, pattern=[[1, BE]],
                                        channel_multiplier=-BE).then_inc(masked, 1)
                pool.wait_ge(span_lane, 1)
                nc.gpsimd.partition_all_reduce(span_all[:, :], span1[:, :], P, RMAX).then_inc(span_all_ready, 1)

            @block.tensor
            def _(pe):
                for g in range(NG):
                    n = rows_of[g]
                    pe.wait_ge(indexed, 4 * (g + 1))
                    if g == NG - 1:
                        pe.wait_ge(masked, 1)
                    for t in range(BT):
                        tile = BT * g + t
                        if tile >= 2:
                            pe.wait_ge(taken[t % 2], 2 * (tile // 2))
                        for a in range(4):
                            last = nc.tensor.transpose(ps[t % 2][:, a, 0:n], val[0:n, a, t * P:(t + 1) * P],
                                                       m.ident[0:n, 0:n])
                        last.then_inc(turned, 1)


def load_nodes(eng, sh, dst, dram, loaded):
    whole = sh.N // P
    eng.dma_start(dst[:, 0:whole, :], dram[0:whole * P, :].rearrange("(t p) d -> p t d", p=P)).then_inc(loaded, 16)
    eng.dma_start(dst[0:sh.N - whole * P, whole, :], dram[whole * P:sh.N, :]).then_inc(loaded, 16)


def layernorm_relu(nc, sem, sh, name, h, x, scratch, x_dram=None, h_dram=None):
    cleared, loaded, made, root, kept = (sem(f"{name}_{x}") for x in ("cleared", "loaded", "made", "root", "kept"))
    with ExitStack() as local:
        def sb(what):
            return local.enter_context(nc.sbuf_tensor(f"{name}_{what}", [P, sh.NT], F32))

        mean, var, std, rstd = sb("mean"), sb("var"), sb("std"), sb("rstd")
        wide = [P, sh.NT, D]
        with nc.Block() as block:
            @block.sync
            def _(sp):
                if x_dram is not None:
                    sp.wait_ge(cleared, 1)
                    load_nodes(sp, sh, x, x_dram, loaded)
                if h_dram is not None:
                    sp.wait_ge(made, 7)
                    sp.dma_start(h_dram.rearrange("(t p) d -> p t d", p=P), h[:, :, :]).then_inc(kept, 16)
                    sp.wait_ge(kept, 16)

            @block.vector
            def _(dve):
                v = nc.vector
                if x_dram is not None:
                    v.memset(x[:, sh.N // P:sh.NT, :], 0.0).then_inc(cleared, 1)
                    dve.wait_ge(loaded, 32)
                v.tensor_reduce(mean[:, :], x[:, :, :], AX.X, ALU.add).then_inc(made, 1)
                dve.wait_ge(made, 1)
                v.scalar_tensor_tensor(h[:, :, :], mean[:, :].unsqueeze(2).to_broadcast(wide), -1.0 / D, x[:, :, :],
                                       ALU.mult, ALU.add).then_inc(made, 1)
                dve.wait_ge(made, 2)
                v.tensor_tensor(scratch[:, :, :], h[:, :, :], h[:, :, :], ALU.mult).then_inc(made, 1)
                dve.wait_ge(made, 3)
                v.tensor_reduce(var[:, :], scratch[:, :, :], AX.X, ALU.add).then_inc(made, 1)
                dve.wait_ge(made, 4)
                v.tensor_scalar(std[:, :], var[:, :], 1.0 / D, LN_EPS, ALU.mult, ALU.add).then_inc(made, 1)
                dve.wait_ge(root, 1)
                v.reciprocal(rstd[:, :], std[:, :]).then_inc(made, 1)
                dve.wait_ge(made, 6)
                v.scalar_tensor_tensor(h[:, :, :], h[:, :, :], 0.0, rstd[:, :].unsqueeze(2).to_broadcast(wide),
                                       ALU.max, ALU.mult).then_inc(made, 1)
                dve.wait_ge(made, 7)

            @block.scalar
            def _(act):
                act.wait_ge(made, 5)
                nc.scalar.activation(std[:, :], std[:, :], ACT.Sqrt).then_inc(root, 1)


def relation_table(nc, sem, sh, m, name, table, weights, n_rel, h=None, with_h=False, root=None, bias=None):
    wide = (2 * D) if with_h else D
    off = wide - D
    per_bank = n_rel // 2 if n_rel * D > 512 else n_rel
    banks = n_rel // per_bank
    w_in, staged, turned, ht_ready, projected, rooted = (sem(f"{name}_{x}") for x in (
        "weights", "staged", "turned", "ht", "projected", "rooted"))
    sums_ready, rows_ready, copies_ready = (sem(f"{name}_{x}") for x in ("sums", "rows", "copies"))
    stored = [sem(f"{name}_stored{q}") for q in range(2)]
    n_w = 16 * (1 if root is None else 3)
    with ExitStack() as local:
        def sb(what, shape):
            return local.enter_context(nc.sbuf_tensor(f"{name}_{what}", shape, F32))

        w = sb("w", [D, n_rel, D])
        w_root, b_root = sb("w_root", [D, D]), sb("b_root", [D, 1])
        ht = sb("ht", [D, 2, P])
        h_tile = sb("h_tile", [P, 2, D])
        rows = sb("rows", [P, 2, n_rel, wide])
        ps_t = [local.enter_context(nc.psum_tensor(f"{name}_ps_t{q}", [D, 512], F32)) for q in range(2)]
        ps_w = [[local.enter_context(nc.psum_tensor(f"{name}_ps_w{q}{b}", [P, 512], F32)) for b in range(banks)]
                for q in range(2)]
        ps_r = [local.enter_context(nc.psum_tensor(f"{name}_ps_r{q}", [D, 512], F32)) for q in range(2)] if root is not None else None

        with nc.Block() as block:
            @block.sync
            def _(sp):
                sp.dma_start(w[:, :, :], weights.rearrange("r i o -> i r o")).then_inc(w_in, 16)
                if root is not None:
                    sp.dma_start(w_root[:, :], root).then_inc(w_in, 16)
                    sp.dma_start(b_root[:, :], bias.rearrange("(o a) -> o a", a=1)).then_inc(w_in, 16)

                def step(t):
                    sp.wait_ge(rows_ready, t.count())
                    if with_h:
                        sp.wait_ge(copies_ready, t.count())
                    sp.dma_start(table[bass.ds(t.number * P, P), :, :], rows[:, t.slot, :, :]
                                 ).then_inc(stored[t.slot], 16)

                each_tile(sp, sh, step)
                for s in stored:
                    sp.wait_ge(s, 16 * (sh.NT // 2))

            if h is not None:
                @block.gpsimd
                def _(pool):
                    each_tile(pool, sh, lambda t: stage_tile(
                        nc, pool, sh, m, t, h_tile, h[:, bass.ds(t.number, 1), :].rearrange("p a d -> p (a d)"),
                        staged, turned))

            @block.tensor
            def _(pe):
                pe.wait_ge(w_in, n_w)

                def step(t):
                    if h is not None and t.exists(sh.NT):
                        if t.back(2).exists():
                            pe.wait_ge(ht_ready, t.back(2).count())
                        pe.wait_ge(staged, t.count())
                        hold(pe, m)
                        nc.tensor.transpose(ps_t[t.slot][:, 0:P], h_tile[:, t.slot, :], m.ident[:, :]
                                            ).then_inc(turned, 1)
                    t = t.back(1)
                    if t.exists():
                        pe.wait_ge(ht_ready, t.count())
                        if t.back(2).exists():
                            pe.wait_ge(rows_ready, t.back(2).count())
                        for b in range(banks):
                            last = nc.tensor.matmul(
                                ps_w[t.slot][b][:, 0:per_bank * D], ht[:, t.slot, :],
                                w[:, b * per_bank:(b + 1) * per_bank, :].rearrange("i r o -> i (r o)"),
                                start=True, stop=True)
                        last.then_inc(projected, 1)
                        if root is not None:
                            if t.back(2).exists():
                                pe.wait_ge(sums_ready, t.back(2).count())
                            hold(pe, m)
                            nc.tensor.matmul(ps_r[t.slot][:, 0:P], w_root[:, :], ht[:, t.slot, :],
                                             start=True, stop=True).then_inc(rooted, 1)

                each_tile(pe, sh, step, drain=1)

            @block.scalar
            def _(act):
                if root is not None:
                    act.wait_ge(w_in, n_w)

                def step(t):
                    if t.exists(sh.NT):
                        if t.back(2).exists():
                            act.wait_ge(projected, t.back(2).count())
                            if root is not None:
                                act.wait_ge(rooted, t.back(2).count())
                        cols = bass.ds(t.number * P, P)
                        if h is not None:
                            act.wait_ge(turned, t.count())
                            nc.scalar.copy(ht[:, t.slot, :], ps_t[t.slot][:, 0:P]).then_inc(ht_ready, 1)
                        else:
                            hold(act, m)
                            nc.scalar.activation(ht[:, t.slot, :], m.sums[0:D, cols], ACT.Relu).then_inc(ht_ready, 1)
                        if with_h:
                            if t.back(2).exists():
                                act.wait_ge(stored[t.slot], t.back(2).slot_count(16))
                            hold(act, m)
                            nc.scalar.copy(rows[:, t.slot, :, 0:D], h[:, bass.ds(t.number, 1), :].to_broadcast(
                                [P, n_rel, D])).then_inc(copies_ready, 1)
                    t = t.back(1)
                    if root is not None and t.exists():
                        act.wait_ge(rooted, t.count())
                        hold(act, m)
                        nc.scalar.activation(m.sums[0:D, bass.ds(t.number * P, P)], ps_r[t.slot][:, 0:P],
                                             ACT.Identity, bias=b_root[:, :]).then_inc(sums_ready, 1)

                each_tile(act, sh, step, drain=1 if root is not None else 0)

            @block.vector
            def _(dve):
                def step(t):
                    dve.wait_ge(projected, t.count())
                    if t.back(2).exists():
                        dve.wait_ge(stored[t.slot], t.back(2).slot_count(16))
                    for b in range(banks):
                        last = nc.vector.tensor_copy(
                            rows[:, t.slot, b * per_bank:(b + 1) * per_bank, off:wide],
                            ps_w[t.slot][b][:, 0:per_bank * D].rearrange("p (r o) -> p r o", o=D))
                    last.then_inc(rows_ready, 1)

                each_tile(dve, sh, step)


def hold(eng, m):
    eng.sem_inc(m.held)


def stage_tile(nc, pool, sh, m, t, slots, source, staged, used):
    if t.back(2).exists():
        pool.wait_ge(used, t.back(2).count())
        hold(pool, m)
    nc.gpsimd.tensor_copy(slots[:, t.slot, :], source).then_inc(staged, 1)


def passes_of(eng, m):
    span = eng.value_load(m.span_i[0:1, 0:1], min_val=0, max_val=m.max_span)
    return eng.snap(span // W + 1)


def near_or_far(eng, m, program):
    place = eng.value_load(m.span_i[0:1, 1:2], min_val=0, max_val=m.max_place)
    with eng.If(place < P):
        program(True)
    with eng.Else():
        program(False)


def next_windows(nc, dve, sh, m, moved, j):
    nc.vector.tensor_scalar(m.base_f[:, :], m.base_f[:, :], float(W), float(sh.N), ALU.add, ALU.min
                            ).then_inc(moved, 1)
    nc.vector.tensor_scalar(m.base_i[:, :], m.base_i[:, :], W, sh.N, ALU.add, ALU.min).then_inc(moved, 1)
    dve.wait_ge(moved, (j + 1) * 2)


def first_windows(nc, sem, m, name):
    spread = sem(f"{name}_windows")
    with nc.Block() as block:
        @block.sync
        def _(sp):
            sp.dma_start(m.base_f[:, :], m.base_f_dram.rearrange("b a -> (b a)").partition_broadcast(P)
                         ).then_inc(spread, 16)
            sp.dma_start(m.base_i[:, :], m.base_i_dram.rearrange("b a -> a b")).then_inc(spread, 16)
            sp.wait_ge(spread, 32)


def attention_edges(nc, sem, sh, m, table, edge_attr):
    loaded = [sem(f"att_loaded{q}") for q in range(SLOTS)]
    src_in = [sem(f"att_src_in{q}") for q in range(SLOTS)]
    dst_in = [sem(f"att_dst_in{q}") for q in range(SLOTS)]
    near_in = [sem(f"att_near_in{q}") for q in range(SLOTS)]
    (cleared, place_spread, picked, dst_ready, pre_ready, tanh_ready, prod_ready, score_ready, unlike_ready, masked_ready, lane_max_ready,
     max_turned, node_max_ready, diag_ready, max_spread, new_max_ready, drop_ready, kept_ready, shifted_ready,
     weight_ready, scale_ready, summed, scaled, added, moved) = (sem("att_" + x) for x in (
         "cleared", "place_spread", "picked", "dst", "pre", "tanh", "prod", "score", "unlike", "masked", "lane_max", "max_turned",
         "node_max", "diag", "max_spread", "new_max", "drop", "kept", "shifted", "weight", "scale", "summed",
         "scaled", "added", "moved"))
    flat_table = table.rearrange("n r d -> (n r) d")
    with ExitStack() as local:
        def sb(name, shape, dt=F32):
            return local.enter_context(nc.sbuf_tensor(name, shape, dt))

        def psum(name):
            return [local.enter_context(nc.psum_tensor(f"{name}{q}", [P, 512], F32)) for q in range(2)]

        run_max = sb("run_max", [P, sh.NWIN])
        rows = sb("att_rows", [P, SLOTS, 4, BT], I32)
        place = sb("att_place", [1, SLOTS, BE], BF16)
        near = sb("att_near", [P, SLOTS, BT, D])
        pick = sb("att_pick", [P, 2, BE])
        from_src = sb("from_src", [P, SLOTS, BT, 3 * D])
        from_dst = sb("from_dst", [P, SLOTS, BT, 2 * D])
        edge = sb("edge", [P, SLOTS, BT, D])
        score = sb("score", [P, SLOTS, BT])
        wgt = sb("wgt", [P, SLOTS, BT, W])
        lane_max = sb("lane_max", [P, SLOTS, W])
        node_max = sb("node_max", [W, SLOTS])
        diag = sb("diag", [W, SLOTS, W])
        new_max = sb("new_max", [P, SLOTS, W])
        drop = sb("drop", [P, SLOTS, W])
        ps_turn, ps_spread = (local.enter_context(nc.psum_tensor(n, [P, 512], F32)) for n in ("ps_turn", "ps_spread"))
        ps_place = local.enter_context(nc.psum_tensor("ps_place", [P, BE], F32))
        ps_sum, ps_dst = psum("ps_sum"), psum("ps_dst")

        tiles = [P, BT, W]

        with nc.Block() as block:
            @block.sync
            def _(sp):
                def program(near_by):
                    def step(b):
                        if not b.first_use():
                            sp.wait_ge(masked_ready, b.back(SLOTS).count())
                        sp.dma_start(rows[:, b.slot, :, :].rearrange("p a t -> p (a t)"),
                                     m.rows_dram[bass.ds(b.number, 1), :, :].rearrange("b p c -> p (b c)")
                                     ).then_inc(loaded[b.slot], 16)
                        first = b.number * BE
                        if isinstance(first, int):
                            first = min(first, sh.E - BE)
                        sp.dma_start(edge[:, b.slot, :, :], edge_attr[bass.ds(first, BE), :].rearrange(
                            "(t p) d -> p t d", p=P)).then_inc(loaded[b.slot], 16)
                        if near_by:
                            sp.dma_start(place[:, b.slot, :], m.near_dram[bass.ds(b.number, 1), :]
                                         ).then_inc(near_in[b.slot], 16)
                            _, bases = nc.values_load_multi_w_load_instructions(
                                m.near_base[0:1, bass.ds(b.number * BT, BT)], engines=[mybir.EngineType.SP],
                                min_val=0, max_val=sh.NPAD * sh.R0 - P)
                            for t, base in enumerate(bases):
                                sp.dma_start(near[:, b.slot, t, :], flat_table[bass.ds(base, P), D:2 * D]
                                             ).then_inc(near_in[b.slot], 16)

                    each_block(sp, sh, passes_of(sp, m), step,
                               at_end=lambda j: sp.wait_ge(masked_ready, (j + 1) * sh.NB))

                near_or_far(sp, m, program)

            @block.gpsimd
            def _(pool):
                pool.wait_ge(cleared, 3)

                def program(near_by):
                    def step(b):
                        if not b.first_use():
                            pool.wait_ge(summed, b.back(SLOTS).count())
                        pool.wait_ge(loaded[b.slot], b.slot_count(32))
                        hold(pool, m)
                        if not near_by:
                            for t in range(BT):
                                nc.gpsimd.indirect_dma_start(
                                    out=from_dst[:, b.slot, t, :], out_offset=None, in_=flat_table,
                                    in_offset=bass.IndirectOffsetOnAxis(ap=rows[:, b.slot, 1, t:t + 1], axis=0)
                                ).then_inc(dst_in[b.slot], 16)
                        for t in range(BT):
                            nc.gpsimd.indirect_dma_start(
                                out=from_src[:, b.slot, t, D:3 * D], out_offset=None, in_=flat_table,
                                in_offset=bass.IndirectOffsetOnAxis(ap=rows[:, b.slot, 0, t:t + 1], axis=0)
                            ).then_inc(src_in[b.slot], 16)

                    each_block(pool, sh, passes_of(pool, m), step,
                               at_end=lambda j: pool.wait_ge(summed, (j + 1) * sh.NB))

                near_or_far(pool, m, program)

            @block.vector
            def _(dve):
                v = nc.vector
                v.memset(from_src[:, :, :, 0:D], 1.0).then_inc(cleared, 1)
                v.memset(run_max[:, :], NEG_START).then_inc(cleared, 1)
                v.memset(m.sums[:, :], 0.0).then_inc(cleared, 1)
                dve.wait_ge(cleared, 3)

                def window(b):
                    base = dve.value_load(m.base_i[0:1, bass.ds(b.number, 1)], min_val=0, max_val=sh.N)
                    return bass.ds(base, W)

                def node_maximum(b):
                    dve.wait_ge(max_turned, b.count())
                    v.tensor_reduce(node_max[:, b.slot:b.slot + 1], ps_turn[0:W, 0:P], AX.X, ALU.max
                                    ).then_inc(node_max_ready, 1)
                    dve.wait_ge(node_max_ready, b.count())
                    v.tensor_scalar(diag[:, b.slot, :], m.ident[0:W, 0:W], node_max[:, b.slot:b.slot + 1], None,
                                    ALU.mult).then_inc(diag_ready, 1)

                def scores(b):
                    wg = wgt[:, b.slot, :, :]
                    v.scalar_tensor_tensor(wg, rows[:, b.slot, 3, :].bitcast(F32).unsqueeze(2).to_broadcast(tiles),
                                           m.base_f[:, bass.ds(b.number, 1)],
                                           m.iota[:, :].unsqueeze(1).to_broadcast(tiles),
                                           ALU.subtract, ALU.not_equal).then_inc(unlike_ready, 1)
                    dve.wait_ge(tanh_ready, b.count())
                    dve.wait_ge(src_in[b.slot], b.slot_count(16 * BT))
                    e = edge[:, b.slot, :, :]
                    v.tensor_tensor(e, e, from_src[:, b.slot, :, 2 * D:3 * D], ALU.mult).then_inc(prod_ready, 1)
                    dve.wait_ge(prod_ready, b.count())
                    v.tensor_reduce(score[:, b.slot, :], e, AX.X, ALU.add).then_inc(score_ready, 1)
                    dve.wait_ge(score_ready, b.count())
                    dve.wait_ge(unlike_ready, b.count())
                    v.scalar_tensor_tensor(wg, wg, NEG_MASK, score[:, b.slot, :].unsqueeze(2).to_broadcast(tiles),
                                           ALU.mult, ALU.add).then_inc(masked_ready, 1)
                    dve.wait_ge(masked_ready, b.count())
                    v.tensor_reduce(lane_max[:, b.slot, :], wg.rearrange("p t w -> p w t"), AX.X, ALU.max
                                    ).then_inc(lane_max_ready, 1)

                def add_sums(b):
                    part = m.sums[:, window(b)]
                    if b.back(1).exists():
                        dve.wait_ge(added, b.back(1).count())
                    dve.wait_ge(scale_ready, b.count())
                    v.tensor_tensor(part, part, drop[:, b.slot, :], ALU.mult).then_inc(scaled, 1)
                    dve.wait_ge(scaled, b.count())
                    dve.wait_ge(summed, b.count())
                    v.tensor_tensor(part, part, ps_sum[b.bank][:, 0:W], ALU.add).then_inc(added, 1)

                def new_maximum(b):
                    part = run_max[:, window(b)]
                    if b.back(1).exists():
                        dve.wait_ge(kept_ready, b.back(1).count())
                    dve.wait_ge(max_spread, b.count())
                    v.tensor_tensor(new_max[:, b.slot, :], part, ps_spread[:, 0:W], ALU.max
                                    ).then_inc(new_max_ready, 1)
                    dve.wait_ge(new_max_ready, b.count())
                    v.tensor_tensor(drop[:, b.slot, :], part, new_max[:, b.slot, :], ALU.subtract
                                    ).then_inc(drop_ready, 1)
                    wg = wgt[:, b.slot, :, :]
                    v.tensor_tensor(wg, wg, new_max[:, b.slot, :].unsqueeze(1).to_broadcast(tiles), ALU.subtract
                                    ).then_inc(shifted_ready, 1)
                    dve.wait_ge(drop_ready, b.count())
                    v.tensor_tensor(part, part, new_max[:, b.slot, :], ALU.max).then_inc(kept_ready, 1)

                def pick_rows(b):
                    dve.wait_ge(place_spread, b.count())
                    if b.back(2).exists():
                        dve.wait_ge(dst_ready, b.back(2).count())
                    v.tensor_scalar(pick[:, b.bank, :], ps_place[:, :], m.lane[:, 0:1], None, ALU.is_equal
                                    ).then_inc(picked, 1)

                def before_tanh_near(b):
                    e = edge[:, b.slot, :, :]
                    dve.wait_ge(loaded[b.slot], b.slot_count(32))
                    dve.wait_ge(dst_ready, b.count())
                    v.tensor_tensor(e, e, ps_dst[b.bank][:, :].rearrange("p (t d) -> p t d", d=D), ALU.add
                                    ).then_inc(pre_ready, 1)

                def before_tanh_far(b):
                    e = edge[:, b.slot, :, :]
                    dve.wait_ge(loaded[b.slot], b.slot_count(32))
                    dve.wait_ge(dst_in[b.slot], b.slot_count(16 * BT))
                    v.tensor_tensor(e, e, from_dst[:, b.slot, :, D:2 * D], ALU.add).then_inc(pre_ready, 1)

                def program(near_by):
                    stages = [(node_maximum, 3), (scores, 2), (add_sums, 4), (new_maximum, 3)]
                    stages += [(before_tanh_near, 1), (pick_rows, 0)] if near_by else [(before_tanh_far, 1)]

                    def step(b):
                        for stage, lag in stages:
                            if b.back(lag).exists(sh.NB):
                                stage(b.back(lag))

                    each_block(dve, sh, passes_of(dve, m), step, drain=4, peeled=2,
                               at_end=lambda j: next_windows(nc, dve, sh, m, moved, j))

                near_or_far(dve, m, program)

            @block.scalar
            def _(act):
                def step(b):
                    p = b.back(3)
                    if p.exists():
                        act.wait_ge(shifted_ready, p.count())
                        nc.scalar.activation(wgt[:, p.slot, :, :], wgt[:, p.slot, :, :], ACT.Exp
                                             ).then_inc(weight_ready, 1)
                        act.wait_ge(drop_ready, p.count())
                        nc.scalar.activation(drop[:, p.slot, :], drop[:, p.slot, :], ACT.Exp
                                             ).then_inc(scale_ready, 1)
                    q = b.back(1)
                    if q.exists(sh.NB):
                        act.wait_ge(pre_ready, q.count())
                        nc.scalar.activation(edge[:, q.slot, :, :], edge[:, q.slot, :, :], ACT.Tanh
                                             ).then_inc(tanh_ready, 1)

                each_block(act, sh, passes_of(act, m), step, drain=3)

            @block.tensor
            def _(pe):
                def spread_places(b):
                    pe.wait_ge(near_in[b.slot], b.slot_count(16 * (1 + BT)))
                    if b.back(1).exists():
                        pe.wait_ge(picked, b.back(1).count())
                    half = BE // 2
                    for n in range(2):
                        last = nc.tensor.matmul(ps_place[:, n * half:(n + 1) * half], m.ones_bf[:, :],
                                                place[:, b.slot, n * half:(n + 1) * half], start=True, stop=True)
                    last.then_inc(place_spread, 1)

                def spread_maxima(b):
                    pe.wait_ge(diag_ready, b.count())
                    if b.back(1).exists():
                        pe.wait_ge(new_max_ready, b.back(1).count())
                    nc.tensor.matmul(ps_spread[:, 0:W], m.ones[0:W, :], diag[:, b.slot, :], start=True, stop=True
                                     ).then_inc(max_spread, 1)

                def turn_maxima(b):
                    pe.wait_ge(lane_max_ready, b.count())
                    if b.back(1).exists():
                        pe.wait_ge(node_max_ready, b.back(1).count())
                    hold(pe, m)
                    nc.tensor.transpose(ps_turn[0:W, 0:P], lane_max[:, b.slot, :], m.ident[:, :]
                                        ).then_inc(max_turned, 1)

                def sum_block(b):
                    pe.wait_ge(weight_ready, b.count())
                    if b.back(2).exists():
                        pe.wait_ge(added, b.back(2).count())
                    for t in range(BT):
                        last = nc.tensor.matmul(ps_sum[b.bank][:, 0:W], from_src[:, b.slot, t, 0:2 * D],
                                                wgt[:, b.slot, t, :], start=(t == 0), stop=(t == BT - 1))
                    last.then_inc(summed, 1)

                def pick_dst(b):
                    pe.wait_ge(picked, b.count())
                    if b.back(2).exists():
                        pe.wait_ge(pre_ready, b.back(2).count())
                    for t in range(BT):
                        last = nc.tensor.matmul(ps_dst[b.bank][:, t * D:(t + 1) * D],
                                                pick[:, b.bank, t * P:(t + 1) * P], near[:, b.slot, t, :],
                                                start=True, stop=True)
                    last.then_inc(dst_ready, 1)

                def program(near_by):
                    stages = [(spread_places, 0)] if near_by else []
                    stages += [(spread_maxima, 3), (turn_maxima, 2), (sum_block, 3)]
                    stages += [(pick_dst, 0)] if near_by else []

                    def step(b):
                        for stage, lag in stages:
                            if b.back(lag).exists(sh.NB):
                                stage(b.back(lag))

                    each_block(pe, sh, passes_of(pe, m), step, drain=3, peeled=2)

                near_or_far(pe, m, program)


def attention_output(nc, sem, sh, m, x, h, fc1, fc2):
    (w_zero, w_in, w_turned, w_ready, staged, turned, den_ready, inv_ready, nb_ready, pair_ready, pair_turned, pair_copied,
     mixed, leak_ready, kept, half_ready, x_ready) = (sem("out0_" + x) for x in (
         "w_zero", "w_in", "w_turned", "w_ready", "staged", "turned", "den", "inv", "nb", "pair", "pair_turned",
         "pair_copied", "mixed", "leak", "kept", "half", "x"))
    with ExitStack() as local:
        def sb(name, shape):
            return local.enter_context(nc.sbuf_tensor(name, shape, F32))

        def psum(name):
            return [local.enter_context(nc.psum_tensor(f"{name}{q}", [P, 512], F32)) for q in range(2)]

        w_raw, w = sb("fc_raw", [P, P]), sb("fc", [P, P])
        den, inv = sb("den", [P, 2]), sb("inv", [P, 2])
        nb = sb("nb", [P, 2, D])
        sums_tile = sb("sums_tile", [P, 2, P])
        pair, pair_t = sb("pair", [P, 2, 2 * D]), sb("pair_t", [P, 2, P])
        leak = sb("leak", [P, 2, 2 * D])
        ps_n, ps_p, ps_m = psum("ps_nodes"), psum("ps_pair"), psum("ps_mixed")
        with nc.Block() as block:
            @block.sync
            def _(sp):
                sp.wait_ge(w_zero, 1)
                sp.dma_start(w_raw[0:D, 0:D], fc1).then_inc(w_in, 16)
                sp.dma_start(w_raw[D:P, D:P], fc2).then_inc(w_in, 16)

            @block.gpsimd
            def _(pool):
                each_tile(pool, sh, lambda t: stage_tile(nc, pool, sh, m, t, sums_tile,
                                                         m.sums[:, bass.ds(t.number * P, P)], staged, turned))

            @block.tensor
            def _(pe):
                pe.wait_ge(w_in, 32)
                nc.tensor.transpose(ps_m[0][:, 0:P], w_raw[:, :], m.ident[:, :]).then_inc(w_turned, 1)
                pe.wait_ge(w_ready, 1)

                def step(t):
                    if t.exists(sh.NT):
                        if t.back(2).exists():
                            pe.wait_ge(nb_ready, t.back(2).count())
                        pe.wait_ge(staged, t.count())
                        nc.tensor.transpose(ps_n[t.slot][:, 0:P], sums_tile[:, t.slot, :], m.ident[:, :]
                                            ).then_inc(turned, 1)
                    a = t.back(1)
                    if a.exists(sh.NT):
                        pe.wait_ge(pair_ready, a.count() * 2)
                        if a.back(2).exists():
                            pe.wait_ge(pair_copied, a.back(2).count())
                        nc.tensor.transpose(ps_p[a.slot][:, 0:P], pair[:, a.slot, :], m.ident[:, :]
                                            ).then_inc(pair_turned, 1)
                    b = t.back(2)
                    if b.exists():
                        pe.wait_ge(pair_copied, b.count())
                        if b.back(2).exists():
                            pe.wait_ge(kept, b.back(2).count())
                        nc.tensor.matmul(ps_m[b.slot][:, 0:P], pair_t[:, b.slot, :], w[:, :], start=True, stop=True
                                         ).then_inc(mixed, 1)

                each_tile(pe, sh, step, drain=2, peeled=2)

            @block.scalar
            def _(act):
                act.wait_ge(w_turned, 1)
                nc.scalar.copy(w[:, :], ps_m[0][:, 0:P]).then_inc(w_ready, 1)

                def step(t):
                    a = t.back(1)
                    if a.exists(sh.NT):
                        act.wait_ge(pair_turned, a.count())
                        if a.back(2).exists():
                            act.wait_ge(mixed, a.back(2).count())
                        nc.scalar.copy(pair_t[:, a.slot, :], ps_p[a.slot][:, 0:P]).then_inc(pair_copied, 1)
                    b = t.back(2)
                    if b.exists():
                        act.wait_ge(mixed, b.count())
                        if b.back(2).exists():
                            act.wait_ge(kept, b.back(2).count())
                        nc.scalar.mul(leak[:, b.slot, :], ps_m[b.slot][:, 0:P], LEAK).then_inc(leak_ready, 1)

                each_tile(act, sh, step, drain=2, peeled=2)

            @block.vector
            def _(dve):
                v = nc.vector
                v.memset(w_raw[:, :], 0.0).then_inc(w_zero, 1)

                def neighbours(t):
                    q = t.slot
                    hh = h[:, bass.ds(t.number, 1), :].rearrange("p a d -> p (a d)")
                    dve.wait_ge(turned, t.count())
                    v.tensor_scalar(den[:, q:q + 1], ps_n[q][:, 0:1], TINY, None, ALU.max).then_inc(den_ready, 1)
                    dve.wait_ge(den_ready, t.count())
                    v.reciprocal(inv[:, q:q + 1], den[:, q:q + 1]).then_inc(inv_ready, 1)
                    dve.wait_ge(inv_ready, t.count())
                    v.tensor_scalar(nb[:, q, :], ps_n[q][:, D:2 * D], inv[:, q:q + 1], None, ALU.mult
                                    ).then_inc(nb_ready, 1)
                    dve.wait_ge(nb_ready, t.count())
                    if t.back(2).exists():
                        dve.wait_ge(pair_turned, t.back(2).count())
                    v.tensor_tensor(pair[:, q, 0:D], hh, nb[:, q, :], ALU.add).then_inc(pair_ready, 1)
                    v.tensor_tensor(pair[:, q, D:2 * D], hh, nb[:, q, :], ALU.mult).then_inc(pair_ready, 1)

                def residual(t):
                    q = t.slot
                    xx = x[:, bass.ds(t.number, 1), :].rearrange("p a d -> p (a d)")
                    dve.wait_ge(leak_ready, t.count())
                    v.tensor_tensor(leak[:, q, :], leak[:, q, :], ps_m[q][:, 0:P], ALU.max).then_inc(half_ready, 1)
                    dve.wait_ge(half_ready, t.count())
                    v.tensor_tensor(xx, xx, leak[:, q, 0:D], ALU.add).then_inc(x_ready, 1)
                    dve.wait_ge(x_ready, t.count())
                    v.tensor_tensor(xx, xx, leak[:, q, D:2 * D], ALU.add).then_inc(kept, 1)

                def step(t):
                    if t.exists(sh.NT):
                        neighbours(t)
                    if t.back(2).exists():
                        residual(t.back(2))

                each_tile(dve, sh, step, drain=2, peeled=2)
                dve.wait_ge(kept, sh.NT)


def relation_edges(nc, sem, sh, m, name, table):
    loaded = [sem(f"{name}_loaded{q}") for q in range(SLOTS)]
    src_in = [sem(f"{name}_src_in{q}") for q in range(SLOTS)]
    alike_ready, summed, added, moved = (sem(f"{name}_{x}") for x in (
        "alike", "summed", "added", "moved"))
    flat_table = table.rearrange("n r d -> (n r) d")
    with ExitStack() as local:
        def sb(what, shape, dt=F32):
            return local.enter_context(nc.sbuf_tensor(f"{name}_{what}", shape, dt))

        rows = sb("rows", [P, SLOTS, 4, BT], I32)
        msg = sb("msg", [P, SLOTS, BT, D])
        alike = sb("alike", [P, SLOTS, BT, W])
        ps_sum = [local.enter_context(nc.psum_tensor(f"{name}_ps{q}", [D, 512], F32)) for q in range(2)]
        tiles = [P, BT, W]

        with nc.Block() as block:
            @block.sync
            def _(sp):
                def step(b):
                    if not b.first_use():
                        sp.wait_ge(summed, b.back(SLOTS).count())
                    sp.dma_start(rows[:, b.slot, :, :].rearrange("p a t -> p (a t)"),
                                 m.rows_dram[bass.ds(b.number, 1), :, :].rearrange("b p c -> p (b c)")
                                 ).then_inc(loaded[b.slot], 16)

                each_block(sp, sh, passes_of(sp, m), step, at_end=lambda j: sp.wait_ge(summed, (j + 1) * sh.NB))

            @block.gpsimd
            def _(pool):
                def step(b):
                    if not b.first_use():
                        pool.wait_ge(summed, b.back(SLOTS).count())
                    pool.wait_ge(loaded[b.slot], b.slot_count(16))
                    hold(pool, m)
                    for t in range(BT):
                        nc.gpsimd.indirect_dma_start(
                            out=msg[:, b.slot, t, :], out_offset=None, in_=flat_table,
                            in_offset=bass.IndirectOffsetOnAxis(ap=rows[:, b.slot, 2, t:t + 1], axis=0)
                        ).then_inc(src_in[b.slot], 16)

                each_block(pool, sh, passes_of(pool, m), step,
                           at_end=lambda j: pool.wait_ge(summed, (j + 1) * sh.NB))

            @block.vector
            def _(dve):
                def one_hot(b):
                    dve.wait_ge(loaded[b.slot], b.slot_count(16))
                    nc.vector.scalar_tensor_tensor(
                        alike[:, b.slot, :, :], rows[:, b.slot, 3, :].bitcast(F32).unsqueeze(2).to_broadcast(tiles),
                        m.base_f[:, bass.ds(b.number, 1)], m.iota[:, :].unsqueeze(1).to_broadcast(tiles),
                        ALU.subtract, ALU.is_equal).then_inc(alike_ready, 1)

                def add_sums(b):
                    base = dve.value_load(m.base_i[0:1, bass.ds(b.number, 1)], min_val=0, max_val=sh.N)
                    part = m.sums[0:D, bass.ds(base, W)]
                    if b.back(1).exists():
                        dve.wait_ge(added, b.back(1).count())
                    dve.wait_ge(summed, b.count())
                    nc.vector.tensor_tensor(part, part, ps_sum[b.bank][:, 0:W], ALU.add).then_inc(added, 1)

                def step(b):
                    if b.exists(sh.NB):
                        one_hot(b)
                    if b.back(1).exists():
                        add_sums(b.back(1))

                def end_of_pass(j):
                    next_windows(nc, dve, sh, m, moved, j)

                each_block(dve, sh, passes_of(dve, m), step, drain=1, at_end=end_of_pass)

            @block.tensor
            def _(pe):
                def step(b):
                    pe.wait_ge(alike_ready, b.count())
                    pe.wait_ge(src_in[b.slot], b.slot_count(16 * BT))
                    if b.back(2).exists():
                        pe.wait_ge(added, b.back(2).count())
                    for t in range(BT):
                        last = nc.tensor.matmul(ps_sum[b.bank][:, 0:W], msg[:, b.slot, t, :], alike[:, b.slot, t, :],
                                                start=(t == 0), stop=(t == BT - 1))
                    last.then_inc(summed, 1)

                each_block(pe, sh, passes_of(pe, m), step)


def output(nc, sem, sh, m, x, out):
    staged, turned, ready, stored = (sem("out_" + x) for x in ("staged", "turned", "ready", "stored"))
    with ExitStack() as local:
        sums_tile = local.enter_context(nc.sbuf_tensor("sums_tile_out", [D, 2, P], F32))
        ps = [local.enter_context(nc.psum_tensor(f"out_ps{q}", [P, 512], F32)) for q in range(2)]
        with nc.Block() as block:
            @block.gpsimd
            def _(pool):
                each_tile(pool, sh, lambda t: stage_tile(nc, pool, sh, m, t, sums_tile,
                                                         m.sums[0:D, bass.ds(t.number * P, P)], staged, turned))

            @block.tensor
            def _(pe):
                def step(t):
                    if t.back(2).exists():
                        pe.wait_ge(ready, t.back(2).count())
                    pe.wait_ge(staged, t.count())
                    hold(pe, m)
                    nc.tensor.transpose(ps[t.slot][:, 0:D], sums_tile[:, t.slot, :],
                                        m.ident[0:D, 0:D]).then_inc(turned, 1)

                each_tile(pe, sh, step)

            @block.vector
            def _(dve):
                def step(t):
                    dve.wait_ge(turned, t.count())
                    xx = x[:, bass.ds(t.number, 1), :].rearrange("p a d -> p (a d)")
                    nc.vector.tensor_tensor(xx, xx, ps[t.slot][:, 0:D], ALU.add).then_inc(ready, 1)

                each_tile(dve, sh, step)

            @block.sync
            def _(sp):
                sp.wait_ge(ready, sh.NT)
                whole = sh.N // P
                sp.dma_start(out[0:whole * P, :].rearrange("(t p) d -> p t d", p=P), x[:, 0:whole, :]
                             ).then_inc(stored, 16)
                sp.dma_start(out[whole * P:sh.N, :], x[0:sh.N - whole * P, whole, :]).then_inc(stored, 16)
                sp.wait_ge(stored, 32)


class Shared:
    pass


def build(nc, x, src, dst, edge_attr, type0, type1, w_rel, fc1, fc2, w1, root1, b1, w2, root2, b2, out):
    sh = Shapes(x.shape[0], src.shape[0], w_rel.shape[0], w1.shape[0])
    m = Shared()
    m.max_span = sh.N - 1
    m.max_place = sh.N * sh.R0
    m.rows_dram = nc.dram_tensor("edge_rows", (sh.NB, P, 4 * BT), I32, kind="Internal").ap()
    m.near_dram = nc.dram_tensor("edge_near", (sh.NB, BE), BF16, kind="Internal").ap()
    m.near_base_dram = nc.dram_tensor("near_base_int", (sh.NB, BT), I32, kind="Internal").ap()
    m.base_i_dram = nc.dram_tensor("base_int", (sh.NB, 1), I32, kind="Internal").ap()
    m.base_f_dram = nc.dram_tensor("base_float", (sh.NB, 1), F32, kind="Internal").ap()
    table0 = nc.dram_tensor("table0", (sh.NPAD, sh.R0, 2 * D), F32, kind="Internal").ap()
    table1 = nc.dram_tensor("table1", (sh.NPAD, sh.R1, D), F32, kind="Internal").ap()
    h_dram = nc.dram_tensor("h0", (sh.NPAD, D), F32, kind="Internal").ap()

    with ExitStack() as ctx:
        def sem(name):
            return ctx.enter_context(nc.semaphore(name))

        def sb(name, shape, dt=F32):
            return ctx.enter_context(nc.sbuf_tensor(name, shape, dt))

        m.held = sem("held")
        m.ident, m.ones, m.iota = sb("ident", [P, P]), sb("ones", [P, P]), sb("iota", [P, W])
        m.lane, m.ones_bf = sb("lane", [P, 1]), sb("ones_bf", [1, P], BF16)
        m.base_i, m.base_f = sb("base_i", [1, sh.NB], I32), sb("base_f", [P, sh.NB])
        m.span_i = sb("span_i", [1, 2], I32)
        m.near_base = sb("near_base", [1, sh.NB * BT], I32)
        wide = [P, sh.NT, D]

        constants(nc, sem, m)
        edge_indices(nc, sem, sh, m, src, dst, type0, type1)
        with nc.sbuf_tensor("x_a", wide, F32) as x_a, nc.sbuf_tensor("h_a", wide, F32) as h_a, \
                nc.sbuf_tensor("sq_a", wide, F32) as sq_a:
            layernorm_relu(nc, sem, sh, "ln0", h_a, x_a, sq_a, x_dram=x, h_dram=h_dram)
            relation_table(nc, sem, sh, m, "tab0", table0, w_rel, sh.R0, h=h_a, with_h=True)
        m.sums = sb("sums", [P, sh.NWIN])
        attention_edges(nc, sem, sh, m, table0, edge_attr)

        x_b = sb("x_b", wide)
        with nc.sbuf_tensor("h_b", wide, F32) as h_b, nc.sbuf_tensor("sq_b", wide, F32) as sq_b:
            reloaded = sem("reloaded")
            x_clear = sem("x_clear")
            with nc.Block() as block:
                @block.vector
                def _(dve):
                    nc.vector.memset(x_b[:, sh.N // P:sh.NT, :], 0.0).then_inc(x_clear, 1)

                @block.sync
                def _(sp):
                    sp.dma_start(h_b[:, :, :], h_dram.rearrange("(t p) d -> p t d", p=P)).then_inc(reloaded, 16)
                    sp.wait_ge(x_clear, 1)
                    load_nodes(sp, sh, x_b, x, reloaded)
                    sp.wait_ge(reloaded, 48)
            attention_output(nc, sem, sh, m, x_b, h_b, fc1, fc2)
            layernorm_relu(nc, sem, sh, "ln1", h_b, x_b, sq_b)
            first_windows(nc, sem, m, "conv1")
            relation_table(nc, sem, sh, m, "tab1", table1, w1, sh.R1, h=h_b, root=root1, bias=b1)
        relation_edges(nc, sem, sh, m, "conv1", table1)
        first_windows(nc, sem, m, "conv2")
        relation_table(nc, sem, sh, m, "tab2", table1, w2, sh.R1, root=root2, bias=b2)
        relation_edges(nc, sem, sh, m, "conv2", table1)
        output(nc, sem, sh, m, x_b, out)


_INS = ["x", "src", "dst", "edge_attr_64", "edge_type_10", "edge_type_8", "L0_gnn_relation_weight",
        "L0_gnn_res_fc_w", "L0_gnn_res_fc2_w", "L1_gnn_W1", "L1_gnn_root1", "L1_gnn_b1", "L1_gnn_W2",
        "L1_gnn_root2", "L1_gnn_b2"]


def kernel(**inputs):
    import numpy as _np
    import concourse.bacc as _bacc
    from concourse import mybir as _mybir
    from concourse.bass_utils import run_bass_kernel_spmd as _run

    nc = _bacc.Bacc("TRN2", target_bir_lowering=False, num_devices=1)
    arrays, args = {}, []
    for name in _INS:
        a = _np.ascontiguousarray(inputs[name])
        arrays[f"in_{name}"] = a
        args.append(nc.dram_tensor(f"in_{name}", a.shape, _mybir.dt.from_np(a.dtype), kind="ExternalInput").ap())
    out = nc.dram_tensor("out_0", inputs["x"].shape, _mybir.dt.float32, kind="ExternalOutput").ap()
    build(nc, *args, out)
    r = _run(nc, [arrays], core_ids=[0])
    return r.results[0]["out_0"]
```

```python
from contextlib import ExitStack

import concourse.bass as bass
from concourse import mybir

F32 = mybir.dt.float32
I32 = mybir.dt.int32
BF16 = mybir.dt.bfloat16
ALU = mybir.AluOpType
ACT = mybir.ActivationFunctionType
AX = mybir.AxisListType
RMAX = bass.bass_isa.ReduceOp.max

P = 128
D = 64
GT = 4
BT = 8
BE = BT * P
W = 64
SLOTS = 4
NEG_MASK = -1e30
NEG_START = -1e28
TINY = 1e-30
LN_EPS = 1e-5
LEAK = 0.01


class Shapes:

    def __init__(self, n_nodes, n_edges, r0, r1):
        self.N, self.E, self.R0, self.R1 = n_nodes, n_edges, r0, r1
        self.NG = -(-n_nodes // (GT * P))
        self.NT = self.NG * GT
        self.NPAD = self.NT * P
        self.NWIN = max(self.NPAD, n_nodes + W)
        self.NREAL = -(-n_edges // BE)
        self.OVERLAP = self.NREAL * BE - n_edges
        self.ROUNDS = -(-self.NREAL // SLOTS)
        self.NB = self.ROUNDS * SLOTS


class Item:

    def __init__(self, i, k, slots, done, used, used_less=None):
        self.i, self.k, self.slots, self.done, self.used, self.used_less = i, k, slots, done, used, used_less
        self.slot, self.bank = k % slots, k % 2
        self.number = i * slots + k

    def exists(self, among=None):
        n = self.number
        return not isinstance(n, int) or (n >= 0 and (among is None or n < among))

    def first_use(self):
        return isinstance(self.number, int) and self.number < self.slots

    def is_masked(self, sh):
        return isinstance(self.number, int) and self.number >= max(sh.NREAL, SLOTS)

    def count(self):
        return self.done + (self.k + 1)

    def slot_count(self, each):
        return (self.used + (self.k // self.slots + 1)) * each

    def gathers(self, sh, each):
        last_masked = sh.NB - SLOTS + self.slot >= max(sh.NREAL, SLOTS)
        return ((self.used_less if last_masked else self.used) + (self.k // self.slots + 1)) * each

    def back(self, lag):
        return Item(self.i, self.k - lag, self.slots, self.done, self.used, self.used_less)


def each_block(eng, sh, passes, step, drain=0, peeled=1, at_end=None):
    with eng.Fori(0, passes) as j:
        for i in range(peeled):
            counts = (eng.snap(j * sh.NB + i * SLOTS), eng.snap(j * sh.ROUNDS + i),
                      eng.snap(j * (sh.ROUNDS - 1) + i))
            for k in range(SLOTS):
                step(Item(i, k, SLOTS, *counts))
        with eng.Fori(peeled, sh.ROUNDS - 1) as i:
            counts = (eng.snap(j * sh.NB + i * SLOTS), eng.snap(j * sh.ROUNDS + i),
                      eng.snap(j * (sh.ROUNDS - 1) + i))
            for k in range(SLOTS):
                step(Item(i, k, SLOTS, *counts))
        counts = (eng.snap(j * sh.NB + (sh.NB - SLOTS)), eng.snap(j * sh.ROUNDS + (sh.ROUNDS - 1)),
                  eng.snap(j * (sh.ROUNDS - 1) + (sh.ROUNDS - 1)))
        for k in range(SLOTS + drain):
            step(Item(sh.ROUNDS - 1, k, SLOTS, *counts))
        if at_end:
            at_end(j)


def each_group(eng, sh, step, drain=0, peeled=1, groups=None, between=None, pieces=0):
    n = sh.NG if groups is None else groups
    rounds = n // 2
    peeled = min(peeled, rounds - 1)
    for i in range(peeled):
        for k in range(2):
            step(Item(i, k, 2, i * 2, i))
    done = peeled
    for piece in range(pieces + 1):
        until = max(done, 1 + (rounds - 2) * (piece + 1) // (pieces + 1))
        if until > done:
            with eng.Fori(done, until) as i:
                for k in range(2):
                    step(Item(i, k, 2, i * 2, i))
        done = until
        if piece < pieces:
            between(piece)
    last = rounds - 1
    for k in range(2 + n % 2 + drain):
        step(Item(last, k, 2, last * 2, last))


class Beside:

    def __init__(self, pieces):
        self.pieces = pieces
        self.before, self.piece, self.after = {}, {}, {}

    def start(self, name):
        self.before.get(name, lambda: None)()

    def end(self, name):
        self.after.get(name, lambda: None)()

    def within(self, name):
        return {"between": self.piece.get(name), "pieces": self.pieces}


def constants(nc, sem, m):
    ready = sem("constants_ready")
    with nc.Block() as block:
        @block.gpsimd
        def _(pool):
            nc.gpsimd.memset(m.ident[:, :], 0.0).then_inc(ready, 1)
            pool.wait_ge(ready, 1)
            nc.gpsimd.affine_select(out=m.ident[:, :], in_=m.ident[:, :], compare_op=ALU.not_equal, fill=1.0,
                                    base=0, pattern=[[-1, P]], channel_multiplier=1).then_inc(ready, 1)
            nc.gpsimd.iota(m.iota[:, :], pattern=[[1, W]], base=0, channel_multiplier=0,
                           allow_small_or_imprecise_dtypes=True).then_inc(ready, 1)
            nc.gpsimd.iota(m.lane[:, :], pattern=[[0, 1]], base=0, channel_multiplier=1,
                           allow_small_or_imprecise_dtypes=True).then_inc(ready, 1)
            nc.gpsimd.memset(m.ones[:, :], 1.0).then_inc(ready, 1)
            nc.gpsimd.memset(m.ones_bf[:, :], 1.0).then_inc(ready, 1)
            pool.wait_ge(ready, 6)


def edge_indices(nc, sem, sh, m, local, engines, src, dst, type0, type1):
    NG = -(-sh.NB // P)
    rows_of = [min(P, sh.NB - g * P) for g in range(NG)]
    real_of = [min(n, sh.NREAL - 1 - g * P) for g, n in enumerate(rows_of)]
    loads_of = [4 * ((r > 0) + (n - r)) * 16 for n, r in zip(rows_of, real_of)]
    loaded = [sem(f"idx_loaded{q}") for q in range(2)]
    indexed, masked, turned = sem("idx_made"), sem("idx_masked"), sem("idx_turned")
    taken = [sem("idx_taken_v"), sem("idx_taken_s")]
    stored = [sem(f"idx_stored{q}") for q in range(2)]
    bounds, spans_ready = sem("idx_bounds"), sem("idx_spans")
    near_ready = sem("idx_near")
    span_lane, span_all_ready, span_int, spread = (sem("idx_" + x) for x in (
        "span_lane", "span_all", "span_int", "spread"))

    def sb(name, shape, dt):
        return local.enter_context(nc.sbuf_tensor(name, shape, dt))

    raws = [[sb(f"raw_{n}{q}", [P, BE], I32) for n in ("src", "dst", "type0", "type1")] for q in range(2)]
    vals = [sb(f"val{q}", [P, 4, BE], F32) for q in range(2)]
    turned_rows = [sb(f"rows_i{q}", [P, P, 4, BT], I32) for q in range(2)]
    bmins, bmax = [sb(f"bmin{q}", [P, 1], F32) for q in range(2)], sb("bmax", [P, 1], F32)
    span1, span_all = sb("span1", [P, 2], F32), sb("span_all", [P, 2], F32)
    bmins_i = [sb(f"bmin_i{q}", [P, 1], I32) for q in range(2)]
    spans = sb("spans", [P, 2, NG], F32)
    tbase, tbases_i = sb("tbase", [P, BT], F32), [sb(f"tbase_i{q}", [P, BT], I32) for q in range(2)]
    near, nears_bf = sb("near", [P, BE], F32), [sb(f"near_bf{q}", [P, BE], BF16) for q in range(2)]
    ps = [local.enter_context(nc.psum_tensor(f"ps_turn{n}", [P, 4, P], F32)) for n in range(2)]

    def take(eng, copy, g, t):
        n = rows_of[g]
        eng.wait_ge(turned, BT * g + t + 1)
        rows_i = turned_rows[g % 2]
        if g >= 2:
            eng.wait_ge(stored[g % 2], 80 * (g // 2))
        copy(rows_i[:, 0:n, 0:3, t], ps[t % 2][:, 0:3, 0:n].rearrange("p a b -> p b a")).then_inc(taken[t % 2], 1)
        copy(rows_i[:, 0:n, 3, t].bitcast(F32), ps[t % 2][:, 3, 0:n]).then_inc(taken[t % 2], 1)

    def take_all(eng, copy, g, first):
        for t in range(first, BT, 2):
            take(eng, copy, g, t)

    sp, dve, act, pool, pe = engines
    v = nc.vector
    work = Beside(NG + 1)

    def load(g):
        n, real = rows_of[g], real_of[g]
        if g >= 2:
            sp.wait_ge(indexed, 4 * (g - 1))
        for t, a in zip(raws[g % 2], (src, dst, type0, type1)):
            if real > 0:
                sp.dma_start(t[0:real, :], a[g * P * BE:(g * P + real) * BE].rearrange(
                    "(b e) -> b e", e=BE)).then_inc(loaded[g % 2], 16)
            for row in range(real, n):
                sp.dma_start(t[row:row + 1, :], a[sh.E - BE:sh.E].rearrange("(b e) -> b e", e=BE)
                             ).then_inc(loaded[g % 2], 16)

    def store(g):
        n, q = rows_of[g], g % 2
        sp.wait_ge(near_ready, 5 * (g + 1))
        sp.dma_start(m.near_dram[g * P:g * P + n, :], nears_bf[q][0:n, :]).then_inc(stored[q], 16)
        sp.dma_start(m.near_base_dram[g * P:g * P + n, :], tbases_i[q][0:n, :]).then_inc(stored[q], 16)
        sp.wait_ge(bounds, 2 * (g + 1))
        sp.dma_start(m.base_i_dram[g * P:g * P + n, :], bmins_i[q][0:n, :]).then_inc(stored[q], 16)
        sp.dma_start(m.base_f_dram[g * P:g * P + n, :], bmins[q][0:n, :]).then_inc(stored[q], 16)
        for s in taken:
            sp.wait_ge(s, BT * (g + 1))
        sp.dma_start(m.rows_dram[g * P:g * P + n, :, :].rearrange("b p c -> p b c"),
                     turned_rows[q][:, 0:n, :, :].rearrange("p b a t -> p b (a t)")).then_inc(stored[q], 16)

    def sync_before():
        load(0)
        if NG > 1:
            load(1)

    def sync_piece(g):
        if g:
            store(g - 1)
            if g + 1 < NG:
                load(g + 1)

    def sync_after():
        for q in range(2):
            sp.wait_ge(stored[q], 80 * ((NG + 1 - q) // 2))
        sp.dma_start(m.base_f[:, :], m.base_f_dram.rearrange("b a -> (b a)").partition_broadcast(P)
                     ).then_inc(spread, 16)
        sp.dma_start(m.base_i[:, :], m.base_i_dram.rearrange("b a -> a b")).then_inc(spread, 16)
        sp.dma_start(m.near_base[:, :], m.near_base_dram.rearrange("(a b) t -> a (b t)", a=1)).then_inc(spread, 16)
        sp.wait_ge(spread, 48)

    def vector_before():
        v.memset(spans[:, :, :], 0.0).then_inc(spans_ready, 1)
        dve.wait_ge(spans_ready, 1)

    def index(g):
        n, q = rows_of[g], g % 2
        dve.wait_ge(loaded[q], sum(loads_of[q:g + 1:2]))
        if g >= 2:
            dve.wait_ge(turned, BT * (g - 1))
            dve.wait_ge(stored[q], 80 * (g // 2))
        r_src, r_dst, r_t0, r_t1 = (t[0:n, :] for t in raws[q])
        val, bmin, bmin_i, tbase_i, near_bf = vals[q], bmins[q], bmins_i[q], tbases_i[q], nears_bf[q]
        v.scalar_tensor_tensor(val[0:n, 0, :], r_src, float(sh.R0), r_t0, ALU.mult, ALU.add
                               ).then_inc(indexed, 1)
        v.scalar_tensor_tensor(val[0:n, 1, :], r_dst, float(sh.R0), r_t0, ALU.mult, ALU.add
                               ).then_inc(indexed, 1)
        v.scalar_tensor_tensor(val[0:n, 2, :], r_src, float(sh.R1), r_t1, ALU.mult, ALU.add
                               ).then_inc(indexed, 1)
        v.tensor_copy(val[0:n, 3, :], r_dst).then_inc(indexed, 1)
        dve.wait_ge(indexed, 4 * (g + 1))
        v.tensor_reduce(tbase[0:n, :], val[0:n, 3, :].rearrange("b (t p) -> b t p", p=P), AX.X, ALU.min
                        ).then_inc(near_ready, 1)
        v.tensor_reduce(bmax[0:n, :], val[0:n, 3, :], AX.X, ALU.max).then_inc(spans_ready, 1)
        dve.wait_ge(near_ready, 5 * g + 1)
        v.tensor_reduce(bmin[0:n, :], tbase[0:n, :], AX.X, ALU.min).then_inc(bounds, 1)
        dve.wait_ge(bounds, 2 * g + 1)
        v.tensor_copy(bmin_i[0:n, :], bmin[0:n, :]).then_inc(bounds, 1)
        v.tensor_scalar(tbase[0:n, :], tbase[0:n, :], float(sh.R0), float(sh.NPAD * sh.R0 - P),
                        ALU.mult, ALU.min).then_inc(near_ready, 1)
        dve.wait_ge(near_ready, 5 * g + 2)
        v.tensor_copy(tbase_i[0:n, :], tbase[0:n, :]).then_inc(near_ready, 1)
        v.tensor_tensor(near[0:n, :].rearrange("b (t p) -> b t p", p=P),
                        val[0:n, 1, :].rearrange("b (t p) -> b t p", p=P),
                        tbase[0:n, :].unsqueeze(2).to_broadcast([n, BT, P]), ALU.subtract
                        ).then_inc(near_ready, 1)
        dve.wait_ge(near_ready, 5 * g + 4)
        v.tensor_copy(near_bf[0:n, :], near[0:n, :]).then_inc(near_ready, 1)
        dve.wait_ge(spans_ready, 2 + 3 * g)
        v.tensor_tensor(spans[0:n, 0, g:g + 1], bmax[0:n, :], bmin[0:n, :], ALU.subtract
                        ).then_inc(spans_ready, 1)
        v.tensor_reduce(spans[0:n, 1, g:g + 1], near[0:n, :], AX.X, ALU.max).then_inc(spans_ready, 1)

    def vector_piece(g):
        if g:
            take_all(dve, v.tensor_copy, g - 1, 0)
        if g < NG:
            index(g)

    def vector_after():
        dve.wait_ge(spans_ready, 1 + 3 * NG)
        v.tensor_reduce(span1[:, :], spans[:, :, :], AX.X, ALU.max).then_inc(span_lane, 1)
        dve.wait_ge(span_all_ready, 1)
        v.tensor_copy(m.span_i[:, :], span_all[0:1, :]).then_inc(span_int, 1)
        dve.wait_ge(span_int, 1)

    def scalar_piece(g):
        if g:
            take_all(act, nc.scalar.copy, g - 1, 1)

    def gpsimd_piece(g):
        if g == NG:
            g -= 1
            pool.wait_ge(bounds, 2 * g + 1)
            pool.wait_ge(spans_ready, 2 + 3 * g)
            pool.wait_ge(near_ready, 5 * g + 1)
            part = vals[g % 2][0:rows_of[g], 3, :]
            nc.gpsimd.affine_select(out=part, in_=part, compare_op=ALU.is_ge, fill=-1.0,
                                    base=real_of[g] * BE - sh.OVERLAP, pattern=[[1, BE]],
                                    channel_multiplier=-BE).then_inc(masked, 1)

    def gpsimd_after():
        pool.wait_ge(span_lane, 1)
        nc.gpsimd.partition_all_reduce(span_all[:, :], span1[:, :], P, RMAX).then_inc(span_all_ready, 1)

    def tensor_piece(g):
        if not g:
            return
        g -= 1
        n = rows_of[g]
        pe.wait_ge(indexed, 4 * (g + 1))
        if g == NG - 1:
            pe.wait_ge(masked, 1)
        for t in range(BT):
            tile = BT * g + t
            if tile >= 2:
                pe.wait_ge(taken[t % 2], 2 * (tile // 2))
            for a in range(4):
                last = nc.tensor.transpose(ps[t % 2][:, a, 0:n], vals[g % 2][0:n, a, t * P:(t + 1) * P],
                                           m.ident[0:n, 0:n])
            last.then_inc(turned, 1)

    work.before = {"sync": sync_before, "vector": vector_before}
    work.piece = {"sync": sync_piece, "vector": vector_piece, "scalar": scalar_piece, "gpsimd": gpsimd_piece,
                  "tensor": tensor_piece}
    work.after = {"sync": sync_after, "vector": vector_after, "gpsimd": gpsimd_after}
    return work


def load_nodes(eng, sh, dst, dram, loaded, first=0):
    whole = sh.N // P
    eng.dma_start(dst[:, first:whole, :], dram[first * P:whole * P, :].rearrange("(t p) d -> p t d", p=P)
                  ).then_inc(loaded, 16)
    eng.dma_start(dst[0:sh.N - whole * P, whole, :], dram[whole * P:sh.N, :]).then_inc(loaded, 16)


def layernorm_relu(nc, sem, sh, name, h, x, scratch, x_dram=None):
    by_vector, by_scalar = sem(f"{name}_by_vector"), sem(f"{name}_by_scalar")
    half = sh.NT // 2
    parts = (slice(0, half), slice(half, sh.NT))
    if x_dram is not None:
        loaded = [sem(f"{name}_loaded{c}") for c in range(2)]
    cleared = 1 if x_dram is not None else 0
    summed, centred = (cleared + 1, cleared + 3), (cleared + 2, cleared + 4)
    varied, scaled = (cleared + 6, cleared + 8), (cleared + 10, cleared + 12)
    with ExitStack() as local:
        def sb(what):
            return local.enter_context(nc.sbuf_tensor(f"{name}_{what}", [P, sh.NT], F32))

        mean, var, std, rstd = sb("mean"), sb("var"), sb("std"), sb("rstd")

        def spread(values, c):
            tiles = parts[c].stop - parts[c].start
            return values[:, parts[c]].unsqueeze(2).to_broadcast([P, tiles, D])

        with nc.Block() as block:
            if x_dram is not None:
                @block.sync
                def _(sp):
                    sp.dma_start(x[:, parts[0], :], x_dram[0:half * P, :].rearrange("(t p) d -> p t d", p=P)
                                 ).then_inc(loaded[0], 16)
                    sp.wait_ge(by_vector, cleared)
                    load_nodes(sp, sh, x, x_dram, loaded[1], first=half)

            @block.vector
            def _(dve):
                v = nc.vector
                if x_dram is not None:
                    v.memset(x[:, sh.N // P:sh.NT, :], 0.0).then_inc(by_vector, 1)
                for c, tiles in enumerate(parts):
                    if x_dram is not None:
                        dve.wait_ge(loaded[c], 16 * (c + 1))
                    v.tensor_reduce(mean[:, tiles], x[:, tiles, :], AX.X, ALU.add).then_inc(by_vector, 1)
                    dve.wait_ge(by_vector, summed[c])
                    v.scalar_tensor_tensor(h[:, tiles, :], spread(mean, c), -1.0 / D, x[:, tiles, :],
                                           ALU.mult, ALU.add).then_inc(by_vector, 1)
                for c, tiles in enumerate(parts):
                    dve.wait_ge(by_scalar, c + 1)
                    v.tensor_reduce(var[:, tiles], scratch[:, tiles, :], AX.X, ALU.add).then_inc(by_vector, 1)
                    dve.wait_ge(by_vector, varied[c] - 1)
                    v.tensor_scalar(std[:, tiles], var[:, tiles], 1.0 / D, LN_EPS, ALU.mult, ALU.add
                                    ).then_inc(by_vector, 1)
                for c, tiles in enumerate(parts):
                    dve.wait_ge(by_scalar, c + 3)
                    v.reciprocal(rstd[:, tiles], std[:, tiles]).then_inc(by_vector, 1)
                    dve.wait_ge(by_vector, scaled[c] - 1)
                    v.scalar_tensor_tensor(h[:, tiles, :], h[:, tiles, :], 0.0, spread(rstd, c),
                                           ALU.max, ALU.mult).then_inc(by_vector, 1)
                dve.wait_ge(by_vector, scaled[1])

            @block.scalar
            def _(act):
                for c, tiles in enumerate(parts):
                    act.wait_ge(by_vector, centred[c])
                    nc.scalar.activation(scratch[:, tiles, :], h[:, tiles, :], ACT.Square).then_inc(by_scalar, 1)
                for c, tiles in enumerate(parts):
                    act.wait_ge(by_vector, varied[c])
                    nc.scalar.activation(std[:, tiles], std[:, tiles], ACT.Sqrt).then_inc(by_scalar, 1)


def relation_table(nc, sem, sh, m, name, table, weights, n_rel, h=None, with_h=False, root=None, bias=None,
                   beside=None, h_dram=None):
    wide = (2 * D) if with_h else D
    off = wide - D
    per_bank = n_rel // 2 if n_rel * D > 512 else n_rel
    banks = n_rel // per_bank
    w_in, w_split, tops_ready, rest_ready, mid_ready, low_ready, projected, rows_ready = (
        sem(f"{name}_{x}") for x in ("weights", "w_split", "tops", "rest", "mid", "low", "projected", "rows"))
    staged, turned = (sem(f"{name}_{x}") if h is not None else None for x in ("staged", "turned"))
    rooted, sums_ready = (sem(f"{name}_{x}") if root is not None else None for x in ("rooted", "sums"))
    copies_ready = sem(f"{name}_copies") if with_h else None
    stored = [sem(f"{name}_stored{q}") for q in range(2)]
    h_kept = sem(f"{name}_h_kept") if h_dram is not None else None
    beside = beside or Beside(0)
    n_mat = n_rel + (root is not None)
    with ExitStack() as local:
        def sb(what, shape, dt=F32):
            return local.enter_context(nc.sbuf_tensor(f"{name}_{what}", shape, dt))

        def psum(what, lanes, n):
            return [local.enter_context(nc.psum_tensor(f"{name}_{what}{q}", [lanes, 512], F32)) for q in range(n)]

        w, w_rest = sb("w", [P, n_mat, D]), sb("w_rest", [P, n_mat, D])
        w11, w22, w31 = (sb(n, [P, n_mat, D], BF16) for n in ("w11", "w22", "w31"))
        b_root = sb("b_root", [D, 1])
        h_tile = sb("h_tile", [P, 2, GT, D])
        h12, h13 = (sb(n, [P, 2, GT * P], BF16) for n in ("h12", "h13"))
        h_rest = sb("h_rest", [P, 2, GT * P])
        rows = sb("rows", [P, 2, GT, n_rel, wide])
        ps_t = psum("ps_t", D, 2)
        ps_w = [psum(f"ps_w{u}", P, banks) for u in range(2)]
        ps_r = psum("ps_r", D, 2) if root is not None else None

        def columns(g):
            return bass.ds(g.number * (GT * P), GT * P)

        with nc.Block() as block:
            @block.sync
            def _(sp):
                for half in range(2):
                    lanes = slice(half * D, half * D + D)
                    sp.dma_start(w[lanes, 0:n_rel, :], weights.rearrange("r i o -> i r o")).then_inc(w_in, 16)
                    if root is not None:
                        sp.dma_start(w[lanes, n_rel, :], root).then_inc(w_in, 16)
                if root is not None:
                    sp.dma_start(b_root[:, :], bias.rearrange("(o a) -> o a", a=1)).then_inc(w_in, 16)

                def step(g):
                    g = g.back(1)
                    if not g.exists():
                        return
                    sp.wait_ge(rows_ready, g.count() * GT)
                    if with_h:
                        sp.wait_ge(copies_ready, g.count())
                    sp.dma_start(table[columns(g), :, :].rearrange("(t p) r d -> p t (r d)", p=P),
                                 rows[:, g.slot, :, :, :].rearrange("p t r d -> p t (r d)")
                                 ).then_inc(stored[g.slot], 16)

                beside.start("sync")
                if h_dram is not None:
                    sp.dma_start(h_dram.rearrange("(t p) d -> p t d", p=P), h[:, :, :]).then_inc(h_kept, 16)
                each_group(sp, sh, step, drain=1, **beside.within("sync"))
                sp.wait_ge(stored[0], 16 * ((sh.NG + 1) // 2))
                sp.wait_ge(stored[1], 16 * (sh.NG // 2))
                if h_dram is not None:
                    sp.wait_ge(h_kept, 16)
                beside.end("sync")

            if h is not None:
                @block.gpsimd
                def _(pool):
                    each_group(pool, sh, lambda g: stage_group(
                        nc, pool, sh, m, g, h_tile, h[:, bass.ds(g.number * GT, GT), :], staged, turned),
                        **beside.within("gpsimd"))
                    beside.end("gpsimd")

            @block.tensor
            def _(pe):
                def turn(g):
                    if g.back(2).exists():
                        pe.wait_ge(rest_ready, g.back(2).count())
                    pe.wait_ge(staged, g.count())
                    hold(pe, m)
                    for u in range(GT):
                        last = nc.tensor.transpose(ps_t[g.slot][:, u * P:(u + 1) * P], h_tile[:, g.slot, u, :],
                                                   m.ident[:, :])
                    last.then_inc(turned, 1)

                def project(g):
                    pe.wait_ge(low_ready, g.count())
                    terms = ((h12, w11), (h12, w22), (h13, w31))
                    if root is not None:
                        if g.back(2).exists():
                            pe.wait_ge(sums_ready, g.back(2).count())
                        hold(pe, m)
                        for n, (parts, mats) in enumerate(terms):
                            last = nc.tensor.matmul(ps_r[g.slot][:, :], mats[:, n_rel, :], parts[:, g.slot, :],
                                                    start=(n == 0), stop=(n == 2))
                        last.then_inc(rooted, 1)
                    for u in range(GT):
                        if u >= 2 or g.back(1).exists():
                            pe.wait_ge(rows_ready, (g.done + g.k) * GT + (u - 1))
                        for b in range(banks):
                            for n, (parts, mats) in enumerate(terms):
                                last = nc.tensor.matmul(
                                    ps_w[u % 2][b][:, 0:per_bank * D], parts[:, g.slot, u * P:(u + 1) * P],
                                    mats[:, b * per_bank:(b + 1) * per_bank, :].rearrange("i r o -> i (r o)"),
                                    start=(n == 0), stop=(n == 2))
                        last.then_inc(projected, 1)

                def step(g):
                    if h is not None and g.exists(sh.NG):
                        turn(g)
                    if g.back(1).exists():
                        project(g.back(1))

                pe.wait_ge(w_split, 7)
                each_group(pe, sh, step, drain=1, **beside.within("tensor"))

            @block.scalar
            def _(act):
                if root is not None:
                    act.wait_ge(w_in, 16 * 5)

                def split_tops(g):
                    if g.back(2).exists():
                        act.wait_ge(projected, g.back(2).count() * GT)
                    if h is not None:
                        act.wait_ge(turned, g.count())
                        for parts in (h12, h13):
                            nc.scalar.copy(parts[0:D, g.slot, :], ps_t[g.slot][:, :]).then_inc(tops_ready, 1)
                    else:
                        hold(act, m)
                        for parts in (h12, h13):
                            nc.scalar.activation(parts[0:D, g.slot, :], m.sums[0:D, columns(g)], ACT.Relu
                                                 ).then_inc(tops_ready, 1)

                def split_mid(g):
                    act.wait_ge(rest_ready, g.count())
                    nc.scalar.copy(h12[D:P, g.slot, :], h_rest[D:P, g.slot, :]).then_inc(mid_ready, 1)

                def copy_h(g):
                    if g.back(2).exists():
                        act.wait_ge(stored[g.slot], g.back(2).slot_count(16))
                    hold(act, m)
                    nc.scalar.copy(rows[:, g.slot, :, :, 0:D],
                                   h[:, bass.ds(g.number * GT, GT), :].unsqueeze(2).to_broadcast(
                                       [P, GT, n_rel, D])).then_inc(copies_ready, 1)

                def start_sums(g):
                    act.wait_ge(rooted, g.count())
                    hold(act, m)
                    nc.scalar.activation(m.sums[0:D, columns(g)], ps_r[g.slot][:, :], ACT.Identity,
                                         bias=b_root[:, :]).then_inc(sums_ready, 1)

                def step(g):
                    if g.exists(sh.NG):
                        split_tops(g)
                        split_mid(g)
                    if with_h and g.back(1).exists():
                        copy_h(g.back(1))
                    if root is not None and g.back(1).exists():
                        start_sums(g.back(1))

                each_group(act, sh, step, drain=1, peeled=2, **beside.within("scalar"))

            @block.vector
            def _(dve):
                v = nc.vector

                def split_weights():
                    dve.wait_ge(w_in, 16 * (2 if root is None else 5))
                    v.tensor_copy(w11[:, :, :], w[:, :, :]).then_inc(w_split, 1)
                    dve.wait_ge(w_split, 1)
                    v.tensor_tensor(w_rest[:, :, :], w[:, :, :], w11[:, :, :], ALU.subtract).then_inc(w_split, 1)
                    v.tensor_copy(w31[D:P, :, :], w11[D:P, :, :]).then_inc(w_split, 1)
                    dve.wait_ge(w_split, 2)
                    v.tensor_copy(w22[:, :, :], w_rest[:, :, :]).then_inc(w_split, 1)
                    dve.wait_ge(w_split, 4)
                    v.tensor_tensor(w31[0:D, :, :], w_rest[0:D, :, :], w22[0:D, :, :], ALU.subtract
                                    ).then_inc(w_split, 3)

                def split_rest(g):
                    if g.back(2).exists():
                        dve.wait_ge(low_ready, g.back(2).count())
                    dve.wait_ge(tops_ready, g.count() * 2)
                    if h is not None:
                        v.tensor_tensor(h_rest[D:P, g.slot, :], ps_t[g.slot][:, :], h12[0:D, g.slot, :],
                                        ALU.subtract).then_inc(rest_ready, 1)
                    else:
                        hold(dve, m)
                        v.scalar_tensor_tensor(h_rest[D:P, g.slot, :], m.sums[0:D, columns(g)], 0.0,
                                               h12[0:D, g.slot, :], ALU.max, ALU.subtract).then_inc(rest_ready, 1)

                def split_low(g):
                    dve.wait_ge(mid_ready, g.count())
                    v.tensor_tensor(h13[D:P, g.slot, :], h_rest[D:P, g.slot, :], h12[D:P, g.slot, :], ALU.subtract
                                    ).then_inc(low_ready, 1)

                def copy_rows(g, tiles):
                    if tiles[0] == 0 and g.back(2).exists():
                        dve.wait_ge(stored[g.slot], g.back(2).slot_count(16))
                    for u in tiles:
                        dve.wait_ge(projected, (g.done + g.k) * GT + (u + 1))
                        for b in range(banks):
                            last = v.tensor_copy(
                                rows[:, g.slot, u, b * per_bank:(b + 1) * per_bank, off:wide],
                                ps_w[u % 2][b][:, 0:per_bank * D].rearrange("p (r o) -> p r o", o=D))
                        last.then_inc(rows_ready, 1)

                def step(g):
                    if g.exists(sh.NG):
                        split_rest(g)
                    if g.back(1).exists():
                        copy_rows(g.back(1), (0, 1))
                    if g.exists(sh.NG):
                        split_low(g)
                    if g.back(1).exists():
                        copy_rows(g.back(1), (2, 3))

                split_weights()
                beside.start("vector")
                each_group(dve, sh, step, drain=1, peeled=2, **beside.within("vector"))
                beside.end("vector")


def hold(eng, m):
    eng.sem_inc(m.held)


def stage_group(nc, pool, sh, m, t, slots, source, staged, used):
    if t.back(2).exists():
        pool.wait_ge(used, t.back(2).count())
        hold(pool, m)
    nc.gpsimd.tensor_copy(slots[:, t.slot, :, :], source).then_inc(staged, 1)


def passes_of(eng, m):
    span = eng.value_load(m.span_i[0:1, 0:1], min_val=0, max_val=m.max_span)
    return eng.snap(span // W + 1)


def near_or_far(eng, m, program):
    place = eng.value_load(m.span_i[0:1, 1:2], min_val=0, max_val=m.max_place)
    with eng.If(place < P):
        program(True)
    with eng.Else():
        program(False)


def next_windows(nc, dve, sh, m, moved, j):
    nc.vector.tensor_scalar(m.base_f[:, :], m.base_f[:, :], float(W), float(sh.N), ALU.add, ALU.min
                            ).then_inc(moved, 1)
    nc.vector.tensor_scalar(m.base_i[:, :], m.base_i[:, :], W, sh.N, ALU.add, ALU.min).then_inc(moved, 1)
    dve.wait_ge(moved, (j + 1) * 2)


def first_windows(nc, sem, m, name):
    spread = sem(f"{name}_windows")
    work = Beside(0)

    def start():
        nc.sync.dma_start(m.base_f[:, :], m.base_f_dram.rearrange("b a -> (b a)").partition_broadcast(P)
                          ).then_inc(spread, 16)
        nc.sync.dma_start(m.base_i[:, :], m.base_i_dram.rearrange("b a -> a b")).then_inc(spread, 16)

    work.before["sync"] = start
    work.after["sync"] = lambda: nc.sync.wait_ge(spread, 32)
    return work


def attention_edges(nc, sem, sh, m, table, edge_attr):
    loaded = [sem(f"att_loaded{q}") for q in range(SLOTS)]
    src_in = [sem(f"att_src_in{q}") for q in range(SLOTS)]
    dst_in = [sem(f"att_dst_in{q}") for q in range(SLOTS)]
    near_in = [sem(f"att_near_in{q}") for q in range(SLOTS)]
    (cleared, place_spread, picked, dst_ready, pre_ready, tanh_ready, prod_ready, score_ready, unlike_ready,
     masked_ready, lane_max_ready,
     max_turned, node_max_ready, diag_ready, max_spread, new_max_ready, drop_ready, kept_ready, shifted_ready,
     weight_ready, scale_ready, summed, scaled, added, moved) = (sem("att_" + x) for x in (
         "cleared", "place_spread", "picked", "dst", "pre", "tanh", "prod", "score", "unlike",
         "masked", "lane_max", "max_turned",
         "node_max", "diag", "max_spread", "new_max", "drop", "kept", "shifted", "weight", "scale", "summed",
         "scaled", "added", "moved"))
    flat_table = table.rearrange("n r d -> (n r) d")
    with ExitStack() as local:
        def sb(name, shape, dt=F32):
            return local.enter_context(nc.sbuf_tensor(name, shape, dt))

        def psum(name):
            return [local.enter_context(nc.psum_tensor(f"{name}{q}", [P, 512], F32)) for q in range(2)]

        run_max = sb("run_max", [P, sh.NWIN])
        rows = sb("att_rows", [P, SLOTS, 4, BT], I32)
        place = sb("att_place", [1, SLOTS, BE], BF16)
        near = sb("att_near", [P, SLOTS, BT, D])
        pick = sb("att_pick", [P, 2, BE])
        from_src = sb("from_src", [P, SLOTS, BT, 3 * D])
        from_dst = sb("from_dst", [P, SLOTS, BT, 2 * D])
        edge = sb("edge", [P, SLOTS, BT, D])
        score = sb("score", [P, SLOTS, BT])
        wgt = sb("wgt", [P, SLOTS, BT, W])
        lane_max = sb("lane_max", [P, SLOTS, W])
        node_max = sb("node_max", [W, SLOTS])
        diag = sb("diag", [W, SLOTS, W])
        new_max = sb("new_max", [P, SLOTS, W])
        drop = sb("drop", [P, SLOTS, W])
        ps_turn, ps_spread = (local.enter_context(nc.psum_tensor(n, [P, 512], F32)) for n in ("ps_turn", "ps_spread"))
        ps_place = local.enter_context(nc.psum_tensor("ps_place", [P, BE], F32))
        ps_sum, ps_dst = psum("ps_sum"), psum("ps_dst")

        tiles = [P, BT, W]

        with nc.Block() as block:
            @block.sync
            def _(sp):
                def program(near_by):
                    def step(b):
                        if not b.first_use():
                            sp.wait_ge(masked_ready, b.back(SLOTS).count())
                        sp.dma_start(rows[:, b.slot, :, :].rearrange("p a t -> p (a t)"),
                                     m.rows_dram[bass.ds(b.number, 1), :, :].rearrange("b p c -> p (b c)")
                                     ).then_inc(loaded[b.slot], 16)
                        first = b.number * BE
                        if isinstance(first, int):
                            first = min(first, sh.E - BE)
                        sp.dma_start(edge[:, b.slot, :, :], edge_attr[bass.ds(first, BE), :].rearrange(
                            "(t p) d -> p t d", p=P)).then_inc(loaded[b.slot], 16)
                        if near_by:
                            sp.dma_start(place[:, b.slot, :], m.near_dram[bass.ds(b.number, 1), :]
                                         ).then_inc(near_in[b.slot], 16)
                            _, bases = nc.values_load_multi_w_load_instructions(
                                m.near_base[0:1, bass.ds(b.number * BT, BT)], engines=[mybir.EngineType.SP],
                                min_val=0, max_val=sh.NPAD * sh.R0 - P)
                            for t, base in enumerate(bases):
                                sp.dma_start(near[:, b.slot, t, :], flat_table[bass.ds(base, P), D:2 * D]
                                             ).then_inc(near_in[b.slot], 16)

                    each_block(sp, sh, passes_of(sp, m), step,
                               at_end=lambda j: sp.wait_ge(masked_ready, (j + 1) * sh.NB))

                near_or_far(sp, m, program)

            @block.gpsimd
            def _(pool):
                def program(near_by):
                    def step(b):
                        if not b.first_use():
                            pool.wait_ge(summed, b.back(SLOTS).count())
                        pool.wait_ge(loaded[b.slot], b.slot_count(32))
                        hold(pool, m)
                        if b.is_masked(sh):
                            return
                        if not near_by:
                            for t in range(BT):
                                nc.gpsimd.indirect_dma_start(
                                    out=from_dst[:, b.slot, t, :], out_offset=None, in_=flat_table,
                                    in_offset=bass.IndirectOffsetOnAxis(ap=rows[:, b.slot, 1, t:t + 1], axis=0)
                                ).then_inc(dst_in[b.slot], 16)
                        for t in range(BT):
                            nc.gpsimd.indirect_dma_start(
                                out=from_src[:, b.slot, t, D:3 * D], out_offset=None, in_=flat_table,
                                in_offset=bass.IndirectOffsetOnAxis(ap=rows[:, b.slot, 0, t:t + 1], axis=0)
                            ).then_inc(src_in[b.slot], 16)

                    each_block(pool, sh, passes_of(pool, m), step,
                               at_end=lambda j: pool.wait_ge(summed, (j + 1) * sh.NB))

                near_or_far(pool, m, program)

            @block.vector
            def _(dve):
                v = nc.vector
                v.memset(from_src[:, :, :, 0:D], 1.0).then_inc(cleared, 1)
                v.memset(run_max[:, :], NEG_START).then_inc(cleared, 1)
                v.memset(m.sums[:, :], 0.0).then_inc(cleared, 1)
                dve.wait_ge(cleared, 3)

                def window(b):
                    base = dve.value_load(m.base_i[0:1, bass.ds(b.number, 1)], min_val=0, max_val=sh.N)
                    return bass.ds(base, W)

                def node_maximum(b):
                    dve.wait_ge(max_turned, b.count())
                    v.tensor_reduce(node_max[:, b.slot:b.slot + 1], ps_turn[0:W, 0:P], AX.X, ALU.max
                                    ).then_inc(node_max_ready, 1)
                    dve.wait_ge(node_max_ready, b.count())
                    v.tensor_scalar(diag[:, b.slot, :], m.ident[0:W, 0:W], node_max[:, b.slot:b.slot + 1], None,
                                    ALU.mult).then_inc(diag_ready, 1)

                def scores(b):
                    wg = wgt[:, b.slot, :, :]
                    v.scalar_tensor_tensor(wg, rows[:, b.slot, 3, :].bitcast(F32).unsqueeze(2).to_broadcast(tiles),
                                           m.base_f[:, bass.ds(b.number, 1)],
                                           m.iota[:, :].unsqueeze(1).to_broadcast(tiles),
                                           ALU.subtract, ALU.not_equal).then_inc(unlike_ready, 1)
                    dve.wait_ge(tanh_ready, b.count())
                    if not b.is_masked(sh):
                        dve.wait_ge(src_in[b.slot], b.gathers(sh, 16 * BT))
                    e = edge[:, b.slot, :, :]
                    v.tensor_tensor(e, e, from_src[:, b.slot, :, 2 * D:3 * D], ALU.mult).then_inc(prod_ready, 1)
                    dve.wait_ge(prod_ready, b.count())
                    v.tensor_reduce(score[:, b.slot, :], e, AX.X, ALU.add).then_inc(score_ready, 1)
                    dve.wait_ge(score_ready, b.count())
                    dve.wait_ge(unlike_ready, b.count())
                    v.scalar_tensor_tensor(wg, wg, NEG_MASK, score[:, b.slot, :].unsqueeze(2).to_broadcast(tiles),
                                           ALU.mult, ALU.add).then_inc(masked_ready, 1)
                    dve.wait_ge(masked_ready, b.count())
                    v.tensor_reduce(lane_max[:, b.slot, :], wg.rearrange("p t w -> p w t"), AX.X, ALU.max
                                    ).then_inc(lane_max_ready, 1)

                def add_sums(b):
                    part = m.sums[:, window(b)]
                    if b.back(1).exists():
                        dve.wait_ge(added, b.back(1).count())
                    dve.wait_ge(scale_ready, b.count())
                    v.tensor_tensor(part, part, drop[:, b.slot, :], ALU.mult).then_inc(scaled, 1)
                    dve.wait_ge(scaled, b.count())
                    dve.wait_ge(summed, b.count())
                    v.tensor_tensor(part, part, ps_sum[b.bank][:, 0:W], ALU.add).then_inc(added, 1)

                def new_maximum(b):
                    part = run_max[:, window(b)]
                    if b.back(1).exists():
                        dve.wait_ge(kept_ready, b.back(1).count())
                    dve.wait_ge(max_spread, b.count())
                    v.tensor_tensor(new_max[:, b.slot, :], part, ps_spread[:, 0:W], ALU.max
                                    ).then_inc(new_max_ready, 1)
                    dve.wait_ge(new_max_ready, b.count())
                    v.tensor_tensor(drop[:, b.slot, :], part, new_max[:, b.slot, :], ALU.subtract
                                    ).then_inc(drop_ready, 1)
                    wg = wgt[:, b.slot, :, :]
                    v.tensor_tensor(wg, wg, new_max[:, b.slot, :].unsqueeze(1).to_broadcast(tiles), ALU.subtract
                                    ).then_inc(shifted_ready, 1)
                    dve.wait_ge(drop_ready, b.count())
                    v.tensor_tensor(part, part, new_max[:, b.slot, :], ALU.max).then_inc(kept_ready, 1)

                def pick_rows(b):
                    dve.wait_ge(place_spread, b.count())
                    if b.back(2).exists():
                        dve.wait_ge(dst_ready, b.back(2).count())
                    v.tensor_scalar(pick[:, b.bank, :], ps_place[:, :], m.lane[:, 0:1], None, ALU.is_equal
                                    ).then_inc(picked, 1)

                def before_tanh_near(b):
                    e = edge[:, b.slot, :, :]
                    dve.wait_ge(loaded[b.slot], b.slot_count(32))
                    dve.wait_ge(dst_ready, b.count())
                    v.tensor_tensor(e, e, ps_dst[b.bank][:, :].rearrange("p (t d) -> p t d", d=D), ALU.add
                                    ).then_inc(pre_ready, 1)

                def before_tanh_far(b):
                    e = edge[:, b.slot, :, :]
                    dve.wait_ge(loaded[b.slot], b.slot_count(32))
                    if not b.is_masked(sh):
                        dve.wait_ge(dst_in[b.slot], b.gathers(sh, 16 * BT))
                    v.tensor_tensor(e, e, from_dst[:, b.slot, :, D:2 * D], ALU.add).then_inc(pre_ready, 1)

                def program(near_by):
                    stages = [(node_maximum, 3), (scores, 2), (add_sums, 4), (new_maximum, 3)]
                    stages += [(before_tanh_near, 1), (pick_rows, 0)] if near_by else [(before_tanh_far, 1)]

                    def step(b):
                        for stage, lag in stages:
                            if b.back(lag).exists(sh.NB):
                                stage(b.back(lag))

                    each_block(dve, sh, passes_of(dve, m), step, drain=4, peeled=2,
                               at_end=lambda j: next_windows(nc, dve, sh, m, moved, j))

                near_or_far(dve, m, program)

            @block.scalar
            def _(act):
                def step(b):
                    p = b.back(3)
                    if p.exists():
                        act.wait_ge(shifted_ready, p.count())
                        nc.scalar.activation(wgt[:, p.slot, :, :], wgt[:, p.slot, :, :], ACT.Exp
                                             ).then_inc(weight_ready, 1)
                        act.wait_ge(drop_ready, p.count())
                        nc.scalar.activation(drop[:, p.slot, :], drop[:, p.slot, :], ACT.Exp
                                             ).then_inc(scale_ready, 1)
                    q = b.back(1)
                    if q.exists(sh.NB):
                        act.wait_ge(pre_ready, q.count())
                        nc.scalar.activation(edge[:, q.slot, :, :], edge[:, q.slot, :, :], ACT.Tanh
                                             ).then_inc(tanh_ready, 1)

                each_block(act, sh, passes_of(act, m), step, drain=3)

            @block.tensor
            def _(pe):
                def spread_places(b):
                    pe.wait_ge(near_in[b.slot], b.slot_count(16 * (1 + BT)))
                    if b.back(1).exists():
                        pe.wait_ge(picked, b.back(1).count())
                    half = BE // 2
                    for n in range(2):
                        last = nc.tensor.matmul(ps_place[:, n * half:(n + 1) * half], m.ones_bf[:, :],
                                                place[:, b.slot, n * half:(n + 1) * half], start=True, stop=True)
                    last.then_inc(place_spread, 1)

                def spread_maxima(b):
                    pe.wait_ge(diag_ready, b.count())
                    if b.back(1).exists():
                        pe.wait_ge(new_max_ready, b.back(1).count())
                    nc.tensor.matmul(ps_spread[:, 0:W], m.ones[0:W, :], diag[:, b.slot, :], start=True, stop=True
                                     ).then_inc(max_spread, 1)

                def turn_maxima(b):
                    pe.wait_ge(lane_max_ready, b.count())
                    if b.back(1).exists():
                        pe.wait_ge(node_max_ready, b.back(1).count())
                    hold(pe, m)
                    nc.tensor.transpose(ps_turn[0:W, 0:P], lane_max[:, b.slot, :], m.ident[:, :]
                                        ).then_inc(max_turned, 1)

                def sum_block(b):
                    pe.wait_ge(weight_ready, b.count())
                    if b.back(2).exists():
                        pe.wait_ge(added, b.back(2).count())
                    for t in range(BT):
                        last = nc.tensor.matmul(ps_sum[b.bank][:, 0:W], from_src[:, b.slot, t, 0:2 * D],
                                                wgt[:, b.slot, t, :], start=(t == 0), stop=(t == BT - 1))
                    last.then_inc(summed, 1)

                def pick_dst(b):
                    pe.wait_ge(picked, b.count())
                    if b.back(2).exists():
                        pe.wait_ge(pre_ready, b.back(2).count())
                    for t in range(BT):
                        last = nc.tensor.matmul(ps_dst[b.bank][:, t * D:(t + 1) * D],
                                                pick[:, b.bank, t * P:(t + 1) * P], near[:, b.slot, t, :],
                                                start=True, stop=True)
                    last.then_inc(dst_ready, 1)

                def program(near_by):
                    stages = [(turn_maxima, 2), (sum_block, 3), (spread_maxima, 2)]
                    if near_by:
                        stages = [stages[0], (spread_places, 0), *stages[1:], (pick_dst, 0)]

                    def step(b):
                        for stage, lag in stages:
                            if b.back(lag).exists(sh.NB):
                                stage(b.back(lag))

                    each_block(pe, sh, passes_of(pe, m), step, drain=3, peeled=2)

                near_or_far(pe, m, program)


def attention_output(nc, sem, sh, m, x, h, x_dram, h_dram, fc1, fc2):
    h_loaded, x_loaded = sem("h_reloaded"), sem("x_reloaded")
    (zeroed, w_in, w_turned, w_ready, staged, turned, den_ready, inv_ready, nb_ready, pair_ready, pair_turned,
     pair_copied,
     mixed, leak_ready, kept, half_ready, x_ready) = (sem("out0_" + x) for x in (
         "zeroed", "w_in", "w_turned", "w_ready", "staged", "turned", "den", "inv", "nb", "pair", "pair_turned",
         "pair_copied", "mixed", "leak", "kept", "half", "x"))
    with ExitStack() as local:
        def sb(name, shape):
            return local.enter_context(nc.sbuf_tensor(name, shape, F32))

        def psum(name):
            return [local.enter_context(nc.psum_tensor(f"{name}{q}", [P, 512], F32)) for q in range(2)]

        w_raw, w = sb("fc_raw", [P, P]), sb("fc", [P, P])
        den, inv = sb("den", [P, 2, GT]), sb("inv", [P, 2, GT])
        nb = sb("nb", [P, 2, GT, D])
        sums_tile = sb("sums_tile", [P, 2, GT, P])
        pair, pair_t = sb("pair", [P, 2, GT, 2 * D]), sb("pair_t", [P, 2, GT * P])
        leak = sb("leak", [P, 2, GT, 2 * D])
        ps_n, ps_p, ps_m = psum("ps_nodes"), psum("ps_pair"), psum("ps_mixed")
        with nc.Block() as block:
            @block.sync
            def _(sp):
                sp.wait_ge(zeroed, 2)
                sp.dma_start(w_raw[0:D, 0:D], fc1).then_inc(w_in, 16)
                sp.dma_start(w_raw[D:P, D:P], fc2).then_inc(w_in, 16)
                sp.dma_start(h[:, :, :], h_dram.rearrange("(t p) d -> p t d", p=P)).then_inc(h_loaded, 16)
                load_nodes(sp, sh, x, x_dram, x_loaded)

            @block.gpsimd
            def _(pool):
                each_group(pool, sh, lambda g: stage_group(
                    nc, pool, sh, m, g, sums_tile,
                    m.sums[:, bass.ds(g.number * (GT * P), GT * P)].rearrange("f (t p) -> f t p", p=P), staged, turned))

            @block.tensor
            def _(pe):
                pe.wait_ge(w_in, 32)
                nc.tensor.transpose(ps_m[0][:, 0:P], w_raw[:, :], m.ident[:, :]).then_inc(w_turned, 1)
                pe.wait_ge(w_ready, 1)

                def turn_sums(g):
                    if g.back(2).exists():
                        pe.wait_ge(nb_ready, g.back(2).count())
                    pe.wait_ge(staged, g.count())
                    for u in range(GT):
                        last = nc.tensor.transpose(ps_n[g.slot][:, u * P:(u + 1) * P], sums_tile[:, g.slot, u, :],
                                                   m.ident[:, :])
                    last.then_inc(turned, 1)

                def turn_pairs(g):
                    pe.wait_ge(pair_ready, g.count() * 2)
                    if g.back(2).exists():
                        pe.wait_ge(pair_copied, g.back(2).count())
                    for u in range(GT):
                        last = nc.tensor.transpose(ps_p[g.slot][:, u * P:(u + 1) * P], pair[:, g.slot, u, :],
                                                   m.ident[:, :])
                    last.then_inc(pair_turned, 1)

                def mix(g):
                    pe.wait_ge(pair_copied, g.count())
                    if g.back(2).exists():
                        pe.wait_ge(half_ready, g.back(2).count())
                    for u in range(GT):
                        last = nc.tensor.matmul(ps_m[g.slot][:, u * P:(u + 1) * P],
                                                pair_t[:, g.slot, u * P:(u + 1) * P], w[:, :], start=True, stop=True)
                    last.then_inc(mixed, 1)

                def step(g):
                    for stage, lag in ((turn_sums, 0), (turn_pairs, 1), (mix, 2)):
                        if g.back(lag).exists(sh.NG):
                            stage(g.back(lag))

                each_group(pe, sh, step, drain=2, peeled=2)

            @block.scalar
            def _(act):
                act.wait_ge(w_turned, 1)
                nc.scalar.copy(w[:, :], ps_m[0][:, 0:P]).then_inc(w_ready, 1)

                def copy_pairs(g):
                    act.wait_ge(pair_turned, g.count())
                    if g.back(2).exists():
                        act.wait_ge(mixed, g.back(2).count())
                    nc.scalar.copy(pair_t[:, g.slot, :], ps_p[g.slot][:, :]).then_inc(pair_copied, 1)

                def leaks(g):
                    act.wait_ge(mixed, g.count())
                    if g.back(2).exists():
                        act.wait_ge(kept, g.back(2).count())
                    nc.scalar.mul(leak[:, g.slot, :, :].rearrange("p t d -> p (t d)"), ps_m[g.slot][:, :], LEAK
                                  ).then_inc(leak_ready, 1)

                def step(g):
                    for stage, lag in ((copy_pairs, 1), (leaks, 2)):
                        if g.back(lag).exists(sh.NG):
                            stage(g.back(lag))

                each_group(act, sh, step, drain=2, peeled=2)

            @block.vector
            def _(dve):
                v = nc.vector
                v.memset(w_raw[:, :], 0.0).then_inc(zeroed, 1)
                v.memset(x[:, sh.N // P:sh.NT, :], 0.0).then_inc(zeroed, 1)

                def neighbours(g):
                    q = g.slot
                    hh = h[:, bass.ds(g.number * GT, GT), :]
                    sums = ps_n[q][:, :].rearrange("p (t f) -> p t f", t=GT)
                    dve.wait_ge(turned, g.count())
                    v.tensor_scalar(den[:, q, :], sums[:, :, 0], TINY, None, ALU.max).then_inc(den_ready, 1)
                    dve.wait_ge(den_ready, g.count())
                    v.reciprocal(inv[:, q, :], den[:, q, :]).then_inc(inv_ready, 1)
                    dve.wait_ge(inv_ready, g.count())
                    v.tensor_tensor(nb[:, q, :, :], sums[:, :, D:2 * D],
                                    inv[:, q, :].unsqueeze(2).to_broadcast([P, GT, D]), ALU.mult).then_inc(nb_ready, 1)
                    dve.wait_ge(nb_ready, g.count())
                    if g.back(2).exists():
                        dve.wait_ge(pair_turned, g.back(2).count())
                    v.tensor_tensor(pair[:, q, :, 0:D], hh, nb[:, q, :, :], ALU.add).then_inc(pair_ready, 1)
                    v.tensor_tensor(pair[:, q, :, D:2 * D], hh, nb[:, q, :, :], ALU.mult).then_inc(pair_ready, 1)

                def residual(g):
                    q = g.slot
                    if not g.back(1).exists():
                        dve.wait_ge(x_loaded, 32)
                    xx = x[:, bass.ds(g.number * GT, GT), :]
                    dve.wait_ge(leak_ready, g.count())
                    v.tensor_tensor(leak[:, q, :, :], leak[:, q, :, :], ps_m[q][:, :].rearrange(
                        "p (t f) -> p t f", t=GT), ALU.max).then_inc(half_ready, 1)
                    dve.wait_ge(half_ready, g.count())
                    v.tensor_tensor(xx, xx, leak[:, q, :, 0:D], ALU.add).then_inc(x_ready, 1)
                    dve.wait_ge(x_ready, g.count())
                    v.tensor_tensor(xx, xx, leak[:, q, :, D:2 * D], ALU.add).then_inc(kept, 1)

                def step(g):
                    for stage, lag in ((neighbours, 0), (residual, 2)):
                        if g.back(lag).exists(sh.NG):
                            stage(g.back(lag))

                dve.wait_ge(h_loaded, 16)
                each_group(dve, sh, step, drain=2, peeled=2)
                dve.wait_ge(kept, sh.NG)


def relation_edges(nc, sem, sh, m, name, table):
    loaded = [sem(f"{name}_loaded{q}") for q in range(SLOTS)]
    src_in = [sem(f"{name}_src_in{q}") for q in range(SLOTS)]
    alike_ready, summed, added, moved = (sem(f"{name}_{x}") for x in (
        "alike", "summed", "added", "moved"))
    flat_table = table.rearrange("n r d -> (n r) d")
    with ExitStack() as local:
        def sb(what, shape, dt=F32):
            return local.enter_context(nc.sbuf_tensor(f"{name}_{what}", shape, dt))

        rows = sb("rows", [P, SLOTS, 4, BT], I32)
        msg = sb("msg", [P, SLOTS, BT, D])
        alike = sb("alike", [P, SLOTS, BT, W])
        ps_sum = [local.enter_context(nc.psum_tensor(f"{name}_ps{q}", [D, 512], F32)) for q in range(2)]
        tiles = [P, BT, W]

        with nc.Block() as block:
            @block.sync
            def _(sp):
                def step(b):
                    if not b.first_use():
                        sp.wait_ge(summed, b.back(SLOTS).count())
                    sp.dma_start(rows[:, b.slot, :, :].rearrange("p a t -> p (a t)"),
                                 m.rows_dram[bass.ds(b.number, 1), :, :].rearrange("b p c -> p (b c)")
                                 ).then_inc(loaded[b.slot], 16)

                each_block(sp, sh, passes_of(sp, m), step, at_end=lambda j: sp.wait_ge(summed, (j + 1) * sh.NB))

            @block.gpsimd
            def _(pool):
                def step(b):
                    if not b.first_use():
                        pool.wait_ge(summed, b.back(SLOTS).count())
                    pool.wait_ge(loaded[b.slot], b.slot_count(16))
                    hold(pool, m)
                    if b.is_masked(sh):
                        return
                    for t in range(BT):
                        nc.gpsimd.indirect_dma_start(
                            out=msg[:, b.slot, t, :], out_offset=None, in_=flat_table,
                            in_offset=bass.IndirectOffsetOnAxis(ap=rows[:, b.slot, 2, t:t + 1], axis=0)
                        ).then_inc(src_in[b.slot], 16)

                each_block(pool, sh, passes_of(pool, m), step,
                           at_end=lambda j: pool.wait_ge(summed, (j + 1) * sh.NB))

            @block.vector
            def _(dve):
                def one_hot(b):
                    dve.wait_ge(loaded[b.slot], b.slot_count(16))
                    nc.vector.scalar_tensor_tensor(
                        alike[:, b.slot, :, :], rows[:, b.slot, 3, :].bitcast(F32).unsqueeze(2).to_broadcast(tiles),
                        m.base_f[:, bass.ds(b.number, 1)], m.iota[:, :].unsqueeze(1).to_broadcast(tiles),
                        ALU.subtract, ALU.is_equal).then_inc(alike_ready, 1)

                def add_sums(b):
                    base = dve.value_load(m.base_i[0:1, bass.ds(b.number, 1)], min_val=0, max_val=sh.N)
                    part = m.sums[0:D, bass.ds(base, W)]
                    if b.back(1).exists():
                        dve.wait_ge(added, b.back(1).count())
                    dve.wait_ge(summed, b.count())
                    nc.vector.tensor_tensor(part, part, ps_sum[b.bank][:, 0:W], ALU.add).then_inc(added, 1)

                def step(b):
                    if b.exists(sh.NB):
                        one_hot(b)
                    if b.back(1).exists():
                        add_sums(b.back(1))

                def end_of_pass(j):
                    next_windows(nc, dve, sh, m, moved, j)

                each_block(dve, sh, passes_of(dve, m), step, drain=1, at_end=end_of_pass)

            @block.tensor
            def _(pe):
                def step(b):
                    pe.wait_ge(alike_ready, b.count())
                    if not b.is_masked(sh):
                        pe.wait_ge(src_in[b.slot], b.gathers(sh, 16 * BT))
                    if b.back(2).exists():
                        pe.wait_ge(added, b.back(2).count())
                    for t in range(BT):
                        last = nc.tensor.matmul(ps_sum[b.bank][:, 0:W], msg[:, b.slot, t, :], alike[:, b.slot, t, :],
                                                start=(t == 0), stop=(t == BT - 1))
                    last.then_inc(summed, 1)

                each_block(pe, sh, passes_of(pe, m), step)


def output(nc, sem, sh, m, x, out):
    staged, turned, ready, stored = (sem("out_" + x) for x in ("staged", "turned", "ready", "stored"))
    whole = sh.N // (GT * P)
    with ExitStack() as local:
        sums_tile = local.enter_context(nc.sbuf_tensor("sums_tile_out", [D, 2, GT, P], F32))
        ps = [local.enter_context(nc.psum_tensor(f"out_ps{q}", [P, 512], F32)) for q in range(2)]
        with nc.Block() as block:
            @block.gpsimd
            def _(pool):
                each_group(pool, sh, lambda g: stage_group(
                    nc, pool, sh, m, g, sums_tile,
                    m.sums[0:D, bass.ds(g.number * (GT * P), GT * P)].rearrange("f (t p) -> f t p", p=P),
                    staged, turned))

            @block.tensor
            def _(pe):
                def step(g):
                    if g.back(2).exists():
                        pe.wait_ge(ready, g.back(2).count())
                    pe.wait_ge(staged, g.count())
                    hold(pe, m)
                    for u in range(GT):
                        last = nc.tensor.transpose(ps[g.slot][:, u * D:(u + 1) * D], sums_tile[:, g.slot, u, :],
                                                   m.ident[0:D, 0:D])
                    last.then_inc(turned, 1)

                each_group(pe, sh, step)

            @block.vector
            def _(dve):
                def step(g):
                    dve.wait_ge(turned, g.count())
                    xx = x[:, bass.ds(g.number * GT, GT), :]
                    nc.vector.tensor_tensor(xx, xx, ps[g.slot][:, 0:GT * D].rearrange("p (t d) -> p t d", d=D),
                                            ALU.add).then_inc(ready, 1)

                each_group(dve, sh, step)

            @block.sync
            def _(sp):
                def step(g):
                    sp.wait_ge(ready, g.count())
                    sp.dma_start(out[bass.ds(g.number * (GT * P), GT * P), :].rearrange("(t p) d -> p t d", p=P),
                                 x[:, bass.ds(g.number * GT, GT), :]).then_inc(stored, 16)

                each_group(sp, sh, step, groups=whole)
                sp.wait_ge(ready, sh.NG)
                tiles, dmas = sh.N // P, whole
                if tiles > whole * GT:
                    sp.dma_start(out[whole * GT * P:tiles * P, :].rearrange("(t p) d -> p t d", p=P),
                                 x[:, whole * GT:tiles, :]).then_inc(stored, 16)
                    dmas += 1
                if sh.N > tiles * P:
                    sp.dma_start(out[tiles * P:sh.N, :], x[0:sh.N - tiles * P, tiles, :]).then_inc(stored, 16)
                    dmas += 1
                sp.wait_ge(stored, 16 * dmas)


class Shared:
    pass


def build(nc, x, src, dst, edge_attr, type0, type1, w_rel, fc1, fc2, w1, root1, b1, w2, root2, b2, out):
    sh = Shapes(x.shape[0], src.shape[0], w_rel.shape[0], w1.shape[0])
    m = Shared()
    m.max_span = sh.N - 1
    m.max_place = sh.N * sh.R0
    m.rows_dram = nc.dram_tensor("edge_rows", (sh.NB, P, 4 * BT), I32, kind="Internal").ap()
    m.near_dram = nc.dram_tensor("edge_near", (sh.NB, BE), BF16, kind="Internal").ap()
    m.near_base_dram = nc.dram_tensor("near_base_int", (sh.NB, BT), I32, kind="Internal").ap()
    m.base_i_dram = nc.dram_tensor("base_int", (sh.NB, 1), I32, kind="Internal").ap()
    m.base_f_dram = nc.dram_tensor("base_float", (sh.NB, 1), F32, kind="Internal").ap()
    table0 = nc.dram_tensor("table0", (sh.NPAD, sh.R0, 2 * D), F32, kind="Internal").ap()
    table1 = nc.dram_tensor("table1", (sh.NPAD, sh.R1, D), F32, kind="Internal").ap()
    h_dram = nc.dram_tensor("h0", (sh.NPAD, D), F32, kind="Internal").ap()

    with ExitStack() as ctx:
        def sem(name):
            return ctx.enter_context(nc.semaphore(name))

        def sb(name, shape, dt=F32):
            return ctx.enter_context(nc.sbuf_tensor(name, shape, dt))

        m.held = sem("held")
        m.ident, m.ones, m.iota = sb("ident", [P, P]), sb("ones", [P, P]), sb("iota", [P, W])
        m.lane, m.ones_bf = sb("lane", [P, 1]), sb("ones_bf", [1, P], BF16)
        m.base_i, m.base_f = sb("base_i", [1, sh.NB], I32), sb("base_f", [P, sh.NB])
        m.span_i = sb("span_i", [1, 2], I32)
        m.near_base = sb("near_base", [1, sh.NB * BT], I32)
        wide = [P, sh.NT, D]

        constants(nc, sem, m)
        with nc.sbuf_tensor("h_a", wide, F32) as h_a:
            with nc.sbuf_tensor("x_a", wide, F32) as x_a, nc.sbuf_tensor("sq_a", wide, F32) as sq_a:
                layernorm_relu(nc, sem, sh, "ln0", h_a, x_a, sq_a, x_dram=x)
            with ExitStack() as local:
                engines = (nc.sync, nc.vector, nc.scalar, nc.gpsimd, nc.tensor)
                indices = edge_indices(nc, sem, sh, m, local, engines, src, dst, type0, type1)
                relation_table(nc, sem, sh, m, "tab0", table0, w_rel, sh.R0, h=h_a, with_h=True, beside=indices,
                               h_dram=h_dram)
        m.sums = sb("sums", [P, sh.NWIN])
        attention_edges(nc, sem, sh, m, table0, edge_attr)

        x_b = sb("x_b", wide)
        with nc.sbuf_tensor("h_b", wide, F32) as h_b, nc.sbuf_tensor("sq_b", wide, F32) as sq_b:
            attention_output(nc, sem, sh, m, x_b, h_b, x, h_dram, fc1, fc2)
            layernorm_relu(nc, sem, sh, "ln1", h_b, x_b, sq_b)
            relation_table(nc, sem, sh, m, "tab1", table1, w1, sh.R1, h=h_b, root=root1, bias=b1,
                           beside=first_windows(nc, sem, m, "conv1"))
        relation_edges(nc, sem, sh, m, "conv1", table1)
        relation_table(nc, sem, sh, m, "tab2", table1, w2, sh.R1, root=root2, bias=b2,
                       beside=first_windows(nc, sem, m, "conv2"))
        relation_edges(nc, sem, sh, m, "conv2", table1)
        output(nc, sem, sh, m, x_b, out)


_INS = ["x", "src", "dst", "edge_attr_64", "edge_type_10", "edge_type_8", "L0_gnn_relation_weight",
        "L0_gnn_res_fc_w", "L0_gnn_res_fc2_w", "L1_gnn_W1", "L1_gnn_root1", "L1_gnn_b1", "L1_gnn_W2",
        "L1_gnn_root2", "L1_gnn_b2"]


def kernel(**inputs):
    import numpy as _np
    import concourse.bacc as _bacc
    from concourse import mybir as _mybir
    from concourse.bass_utils import run_bass_kernel_spmd as _run

    nc = _bacc.Bacc("TRN2", target_bir_lowering=False, num_devices=1)
    arrays, args = {}, []
    for name in _INS:
        a = _np.ascontiguousarray(inputs[name])
        arrays[f"in_{name}"] = a
        args.append(nc.dram_tensor(f"in_{name}", a.shape, _mybir.dt.from_np(a.dtype), kind="ExternalInput").ap())
    out = nc.dram_tensor("out_0", inputs["x"].shape, _mybir.dt.float32, kind="ExternalOutput").ap()
    build(nc, *args, out)
    r = _run(nc, [arrays], core_ids=[0])
    return r.results[0]["out_0"]
```
